# Optimizing a Trainium2 kernel written in Bass

```python
import numpy as np
import jax
import jax.numpy as jnp

def _softmax(x, axis=-1):
    return jax.nn.softmax(x, axis=axis)

def _gelu(x):
    return jax.nn.gelu(x, approximate=True)

def _silu(x):
    return jax.nn.silu(x)

def _sigmoid(x):
    return jax.nn.sigmoid(x)

def _layernorm(x, axis=-1, eps=1e-05):
    m = jnp.mean(x, axis=axis, keepdims=True)
    v = jnp.var(x, axis=axis, keepdims=True)
    return (x - m) / jnp.sqrt(v + eps)

def _scatter_add(tgt, idx, src, axis=0):
    return tgt.at[idx].add(src)

def _segment_sum(src, seg, n):
    return jax.ops.segment_sum(src, seg, n)
kernel_name = 'mk_gnn_resnorm_d4_gnn_r32_b66512'

def setup_inputs(seed: int=0):
    np.random.seed(seed)
    _w = jnp.asarray

    def _rec_inputs():
        import jax
        import jax.numpy as jnp
        _gk = jax.random.key(seed)
        x = -0.0003713 + 1 * jax.random.normal(jax.random.fold_in(_gk, 1), (3125, 128), jnp.float32)
        src = jax.random.randint(jax.random.fold_in(_gk, 2), (100000,), 0, 3125, jnp.int32)
        dst = jax.random.randint(jax.random.fold_in(_gk, 3), (100000,), 0, 3125, jnp.int32)
        _o = jnp.argsort(dst, stable=True)
        src = src[_o]
        dst = dst[_o]
        edge_attr_64 = jax.random.uniform(jax.random.fold_in(_gk, 12), (100000, 64), jnp.float32, 0.0, 1)
        return (x, src, dst, edge_attr_64)
    x, src, dst, edge_attr_64 = _rec_inputs()

    def _L0_gnn_setup():
        import jax, jax.numpy as jnp
        import numpy as np
        N_NODES = 3125
        N_EDGES = 50000
        IN_C, HID_C, OUT_C = (128, 256, 128)

        def _gin_conv(x, src, dst, W1, b1, W2, b2):
            agg = jax.ops.segment_sum(x[src], dst, num_segments=N_NODES)
            h = x + agg
            h = jnp.maximum(h @ W1 + b1, 0.0)
            return h @ W2 + b2
        key = jax.random.key(seed)
        ks = jax.random.split(key, 6)
        x = jax.random.normal(ks[0], (N_NODES, IN_C), dtype=jnp.float32)
        edge_index = jax.random.randint(ks[1], (2, N_EDGES), 0, N_NODES, dtype=jnp.int64)
        s = 0.05
        W1a = jax.random.normal(ks[2], (IN_C, HID_C), dtype=jnp.float32) * s
        b1a = jnp.zeros((HID_C,), dtype=jnp.float32)
        W2a = jax.random.normal(ks[3], (HID_C, HID_C), dtype=jnp.float32) * s
        b2a = jnp.zeros((HID_C,), dtype=jnp.float32)
        W1b = jax.random.normal(ks[4], (HID_C, HID_C), dtype=jnp.float32) * s
        b1b = jnp.zeros((HID_C,), dtype=jnp.float32)
        W2b = jax.random.normal(ks[5], (HID_C, OUT_C), dtype=jnp.float32) * s
        b2b = jnp.zeros((OUT_C,), dtype=jnp.float32)
        return {'x': x, 'edge_index': edge_index, 'W1a': W1a, 'b1a': b1a, 'W2a': W2a, 'b2a': b2a, 'W1b': W1b, 'b1b': b1b, 'W2b': W2b, 'b2b': b2b}
    _L0_gnn_all = _L0_gnn_setup()
    _L0_gnn_in = {k: v for k, v in _L0_gnn_all.items() if k in ('W1a', 'b1a', 'W2a', 'b2a', 'W1b', 'b1b', 'W2b', 'b2b')}
    del _L0_gnn_all

    def _L1_gnn_setup():
        import jax, jax.numpy as jnp
        import numpy as np
        N = 50000
        E = 25000
        H = 4
        IN = 128
        C1 = 64
        C2 = 32
        SLOPE = 0.2

        def _supergat_conv(x, src, dst, W, att_l, att_r, bias, heads, ch):
            n = x.shape[0]
            xw = (x @ W).reshape(n, heads, ch)
            xi = xw[dst]
            xj = xw[src]
            logits = jnp.einsum('ehc,ehc->eh', xi, xj)
            alpha = jnp.einsum('ehc,hc->eh', xj, att_l) + jnp.einsum('ehc,hc->eh', xi, att_r)
            alpha = alpha * jax.nn.sigmoid(logits)
            alpha = jnp.where(alpha > 0, alpha, SLOPE * alpha)
            amax = jax.ops.segment_max(alpha, dst, num_segments=n)
            expa = jnp.exp(alpha - amax[dst])
            denom = jax.ops.segment_sum(expa, dst, num_segments=n)
            alpha = expa / (denom[dst] + 1e-16)
            out = jax.ops.segment_sum(xj * alpha[..., None], dst, num_segments=n)
            return out.reshape(n, heads * ch) + bias
        key = jax.random.key(seed)
        ks = jax.random.split(key, 10)
        g = lambda k, shp: jax.random.normal(k, shp, jnp.float32) * 0.05
        x = jax.random.normal(ks[0], (N, IN), jnp.float32)
        edge_index = jax.random.randint(ks[1], (2, E), 0, N, dtype=jnp.int64)
        W1 = g(ks[2], (IN, H * C1))
        att_l1 = g(ks[3], (H, C1))
        att_r1 = g(ks[4], (H, C1))
        b1 = jnp.zeros((H * C1,), jnp.float32)
        W2 = g(ks[5], (H * C1, H * C2))
        att_l2 = g(ks[6], (H, C2))
        att_r2 = g(ks[7], (H, C2))
        b2 = jnp.zeros((H * C2,), jnp.float32)
        return dict(x=x, edge_index=edge_index, W1=W1, att_l1=att_l1, att_r1=att_r1, b1=b1, W2=W2, att_l2=att_l2, att_r2=att_r2, b2=b2)
    _L1_gnn_all = _L1_gnn_setup()
    _L1_gnn_in = {k: v for k, v in _L1_gnn_all.items() if k in ('W1', 'att_l1', 'att_r1', 'b1', 'W2', 'att_l2', 'att_r2', 'b2')}
    del _L1_gnn_all

    def _L2_gnn_setup():
        import jax, jax.numpy as jnp
        import numpy as np
        N_NODES = 50000
        N_EDGES = 25000
        D = 128
        NUM_BLOCKS = 4
        key = jax.random.key(seed)
        ks = jax.random.split(key, 10)
        feat = jax.random.normal(ks[0], (N_NODES, D), dtype=jnp.float32)
        src = jax.random.randint(ks[1], (N_EDGES,), 0, N_NODES, dtype=jnp.int64 if jax.config.jax_enable_x64 else jnp.int32)
        dst = jax.random.randint(ks[2], (N_EDGES,), 0, N_NODES, dtype=jnp.int64 if jax.config.jax_enable_x64 else jnp.int32)
        s = 1.0 / np.sqrt(D)
        gcn_w = jax.random.uniform(ks[3], (NUM_BLOCKS, D, D), jnp.float32, -s, s)
        gcn_b = jnp.zeros((NUM_BLOCKS, D), jnp.float32)
        gru_w_ih = jax.random.uniform(ks[4], (NUM_BLOCKS, 3 * D, D), jnp.float32, -s, s)
        gru_w_hh = jax.random.uniform(ks[5], (NUM_BLOCKS, 3 * D, D), jnp.float32, -s, s)
        gru_b_ih = jax.random.uniform(ks[6], (NUM_BLOCKS, 3 * D), jnp.float32, -s, s)
        gru_b_hh = jax.random.uniform(ks[7], (NUM_BLOCKS, 3 * D), jnp.float32, -s, s)
        return {'feat': feat, 'src': src, 'dst': dst, 'gcn_w': gcn_w, 'gcn_b': gcn_b, 'gru_w_ih': gru_w_ih, 'gru_w_hh': gru_w_hh, 'gru_b_ih': gru_b_ih, 'gru_b_hh': gru_b_hh}
    _L2_gnn_all = _L2_gnn_setup()
    _L2_gnn_in = {k: v for k, v in _L2_gnn_all.items() if k in ('gcn_w', 'gcn_b', 'gru_w_ih', 'gru_w_hh', 'gru_b_ih', 'gru_b_hh')}
    del _L2_gnn_all

    def _L3_gnn_setup():
        import jax, jax.numpy as jnp
        import numpy as np
        N_ATOMS = 625
        N_EDGES = 20000
        N_RBF = 64
        F = 128
        key = jax.random.key(seed)
        ks = jax.random.split(key, 12)
        s = lambda fan_in: 1.0 / np.sqrt(fan_in)
        return {'h': jax.random.normal(ks[0], (N_ATOMS, F), dtype=jnp.float32), 'rbf_ij': jax.random.uniform(ks[1], (N_EDGES, N_RBF), dtype=jnp.float32), 'idx_i': jax.random.randint(ks[2], (N_EDGES,), 0, N_ATOMS), 'idx_j': jax.random.randint(ks[3], (N_EDGES,), 0, N_ATOMS), 'W1': jax.random.normal(ks[4], (N_RBF, F), dtype=jnp.float32) * s(N_RBF), 'b1': jnp.zeros((F,), dtype=jnp.float32), 'W2': jax.random.normal(ks[5], (F, F), dtype=jnp.float32) * s(F), 'b2': jnp.zeros((F,), dtype=jnp.float32), 'W3': jax.random.normal(ks[6], (F, F), dtype=jnp.float32) * s(F), 'b3': jnp.zeros((F,), dtype=jnp.float32), 'W4': jax.random.normal(ks[7], (F, F), dtype=jnp.float32) * s(F), 'b4': jnp.zeros((F,), dtype=jnp.float32)}
    _L3_gnn_all = _L3_gnn_setup()
    _L3_gnn_in = {k: v for k, v in _L3_gnn_all.items() if k in ('W1', 'b1', 'W2', 'b2', 'W3', 'b3', 'W4', 'b4')}
    del _L3_gnn_all
    return {'x': x, 'src': src, 'dst': dst, 'edge_attr_64': edge_attr_64, 'L0_gnn_W1a': _L0_gnn_in['W1a'], 'L0_gnn_b1a': _L0_gnn_in['b1a'], 'L0_gnn_W2a': _L0_gnn_in['W2a'], 'L0_gnn_b2a': _L0_gnn_in['b2a'], 'L0_gnn_W1b': _L0_gnn_in['W1b'], 'L0_gnn_b1b': _L0_gnn_in['b1b'], 'L0_gnn_W2b': _L0_gnn_in['W2b'], 'L0_gnn_b2b': _L0_gnn_in['b2b'], 'L1_gnn_W1': _L1_gnn_in['W1'], 'L1_gnn_att_l1': _L1_gnn_in['att_l1'], 'L1_gnn_att_r1': _L1_gnn_in['att_r1'], 'L1_gnn_b1': _L1_gnn_in['b1'], 'L1_gnn_W2': _L1_gnn_in['W2'], 'L1_gnn_att_l2': _L1_gnn_in['att_l2'], 'L1_gnn_att_r2': _L1_gnn_in['att_r2'], 'L1_gnn_b2': _L1_gnn_in['b2'], 'L2_gnn_gcn_w': _L2_gnn_in['gcn_w'], 'L2_gnn_gcn_b': _L2_gnn_in['gcn_b'], 'L2_gnn_gru_w_ih': _L2_gnn_in['gru_w_ih'], 'L2_gnn_gru_w_hh': _L2_gnn_in['gru_w_hh'], 'L2_gnn_gru_b_ih': _L2_gnn_in['gru_b_ih'], 'L2_gnn_gru_b_hh': _L2_gnn_in['gru_b_hh'], 'L3_gnn_W1': _L3_gnn_in['W1'], 'L3_gnn_b1': _L3_gnn_in['b1'], 'L3_gnn_W2': _L3_gnn_in['W2'], 'L3_gnn_b2': _L3_gnn_in['b2'], 'L3_gnn_W3': _L3_gnn_in['W3'], 'L3_gnn_b3': _L3_gnn_in['b3'], 'L3_gnn_W4': _L3_gnn_in['W4'], 'L3_gnn_b4': _L3_gnn_in['b4']}

def reference(x, src, dst, edge_attr_64, L0_gnn_W1a, L0_gnn_b1a, L0_gnn_W2a, L0_gnn_b2a, L0_gnn_W1b, L0_gnn_b1b, L0_gnn_W2b, L0_gnn_b2b, L1_gnn_W1, L1_gnn_att_l1, L1_gnn_att_r1, L1_gnn_b1, L1_gnn_W2, L1_gnn_att_l2, L1_gnn_att_r2, L1_gnn_b2, L2_gnn_gcn_w, L2_gnn_gcn_b, L2_gnn_gru_w_ih, L2_gnn_gru_w_hh, L2_gnn_gru_b_ih, L2_gnn_gru_b_hh, L3_gnn_W1, L3_gnn_b1, L3_gnn_W2, L3_gnn_b2, L3_gnn_W3, L3_gnn_b3, L3_gnn_W4, L3_gnn_b4):
    import jax
    import jax.numpy as jnp

    def _L0_gnn_ref(x, edge_index, W1a, b1a, W2a, b2a, W1b, b1b, W2b, b2b):
        import jax, jax.numpy as jnp
        import numpy as np
        N_NODES = 3125
        N_EDGES = 50000
        IN_C, HID_C, OUT_C = (128, 256, 128)

        def _gin_conv(x, src, dst, W1, b1, W2, b2):
            agg = jax.ops.segment_sum(x[src], dst, num_segments=N_NODES)
            h = x + agg
            h = jnp.maximum(h @ W1 + b1, 0.0)
            return h @ W2 + b2
        src, dst = (edge_index[0], edge_index[1])
        h = jnp.maximum(_gin_conv(x, src, dst, W1a, b1a, W2a, b2a), 0.0)
        out = _gin_conv(h, src, dst, W1b, b1b, W2b, b2b)
        return out

    def _L1_gnn_ref(x, edge_index, W1, att_l1, att_r1, b1, W2, att_l2, att_r2, b2):
        import jax, jax.numpy as jnp
        import numpy as np
        N = 50000
        E = 25000
        H = 4
        IN = 128
        C1 = 64
        C2 = 32
        SLOPE = 0.2

        def _supergat_conv(x, src, dst, W, att_l, att_r, bias, heads, ch):
            n = x.shape[0]
            xw = (x @ W).reshape(n, heads, ch)
            xi = xw[dst]
            xj = xw[src]
            logits = jnp.einsum('ehc,ehc->eh', xi, xj)
            alpha = jnp.einsum('ehc,hc->eh', xj, att_l) + jnp.einsum('ehc,hc->eh', xi, att_r)
            alpha = alpha * jax.nn.sigmoid(logits)
            alpha = jnp.where(alpha > 0, alpha, SLOPE * alpha)
            amax = jax.ops.segment_max(alpha, dst, num_segments=n)
            expa = jnp.exp(alpha - amax[dst])
            denom = jax.ops.segment_sum(expa, dst, num_segments=n)
            alpha = expa / (denom[dst] + 1e-16)
            out = jax.ops.segment_sum(xj * alpha[..., None], dst, num_segments=n)
            return out.reshape(n, heads * ch) + bias
        n = x.shape[0]
        loops = jnp.arange(n, dtype=edge_index.dtype)
        src = jnp.concatenate([edge_index[0], loops])
        dst = jnp.concatenate([edge_index[1], loops])
        h = jax.nn.elu(_supergat_conv(x, src, dst, W1, att_l1, att_r1, b1, H, C1))
        h = _supergat_conv(h, src, dst, W2, att_l2, att_r2, b2, H, C2)
        return jax.nn.log_softmax(h, axis=1)

    def _L2_gnn_ref(feat, src, dst, gcn_w, gcn_b, gru_w_ih, gru_w_hh, gru_b_ih, gru_b_hh):
        import jax, jax.numpy as jnp
        import numpy as np
        N_NODES = 50000
        N_EDGES = 25000
        D = 128
        NUM_BLOCKS = 4
        n = feat.shape[0]
        ones = jnp.ones(src.shape[0], feat.dtype)
        norm_src = jnp.clip(jax.ops.segment_sum(ones, src, num_segments=n), 1.0) ** (-0.5)
        norm_dst = jnp.clip(jax.ops.segment_sum(ones, dst, num_segments=n), 1.0) ** (-0.5)
        h = feat
        for b in range(NUM_BLOCKS):
            x = h * norm_src[:, None]
            agg = jax.ops.segment_sum(x[src], dst, num_segments=n)
            g = agg * norm_dst[:, None] @ gcn_w[b] + gcn_b[b]
            gi = g @ gru_w_ih[b].T + gru_b_ih[b]
            i_r, i_z, i_n = jnp.split(gi, 3, axis=-1)
            h_r, h_z, h_n = jnp.split(gru_b_hh[b], 3)
            r = jax.nn.sigmoid(i_r + h_r)
            z = jax.nn.sigmoid(i_z + h_z)
            ncand = jnp.tanh(i_n + r * h_n)
            h = jax.nn.relu((1.0 - z) * ncand)
        return h

    def _L3_gnn_ref(h, rbf_ij, idx_i, idx_j, W1, b1, W2, b2, W3, b3, W4, b4):
        import jax, jax.numpy as jnp
        import numpy as np
        N_ATOMS = 625
        N_EDGES = 20000
        N_RBF = 64
        F = 128
        n_atoms = h.shape[0]
        W = jax.nn.silu(rbf_ij @ W1 + b1) @ W2 + b2
        msgs = h[idx_j] * W
        agg = jnp.zeros((n_atoms, h.shape[1]), dtype=h.dtype).at[idx_i].add(msgs)
        delta = jax.nn.silu(agg @ W3 + b3) @ W4 + b4
        return h + delta
    edge_index = jnp.stack([src, dst])
    x = _layernorm(x + _L0_gnn_ref(x, edge_index, L0_gnn_W1a, L0_gnn_b1a, L0_gnn_W2a, L0_gnn_b2a, L0_gnn_W1b, L0_gnn_b1b, L0_gnn_W2b, L0_gnn_b2b), axis=-1)
    x = _layernorm(x + _L1_gnn_ref(x, edge_index, L1_gnn_W1, L1_gnn_att_l1, L1_gnn_att_r1, L1_gnn_b1, L1_gnn_W2, L1_gnn_att_l2, L1_gnn_att_r2, L1_gnn_b2), axis=-1)
    x = _layernorm(x + _L2_gnn_ref(x, src, dst, L2_gnn_gcn_w, L2_gnn_gcn_b, L2_gnn_gru_w_ih, L2_gnn_gru_w_hh, L2_gnn_gru_b_ih, L2_gnn_gru_b_hh), axis=-1)
    x = _layernorm(x + _L3_gnn_ref(x, edge_attr_64, src, dst, L3_gnn_W1, L3_gnn_b1, L3_gnn_W2, L3_gnn_b2, L3_gnn_W3, L3_gnn_b3, L3_gnn_W4, L3_gnn_b4), axis=-1)
    return x

_drawn_inputs = setup_inputs


def setup_inputs(seed=0):
    import zlib

    import numpy as np

    out = dict(_drawn_inputs(seed))
    spreads = {'L0_gnn_b1a': (0.0, 0.313),
     'L0_gnn_b2a': (0.0, 0.1),
     'L0_gnn_b1b': (0.0, 0.8),
     'L0_gnn_b2b': (0.0, 0.8),
     'L1_gnn_b1': (0.0, 0.1),
     'L1_gnn_b2': (0.0, 0.1),
     'L2_gnn_gcn_b': (0.0, 0.354),
     'L3_gnn_b1': (0.0, 0.1),
     'L3_gnn_b2': (0.0, 0.1),
     'L3_gnn_b3': (0.0, 0.8),
     'L3_gnn_b4': (0.0, 0.576)}
    factors = {'L1_gnn_att_l1': 23.029,
     'L1_gnn_att_r1': 35.535,
     'L1_gnn_att_l2': 200.0,
     'L1_gnn_att_r2': 200.0,
     'L2_gnn_gcn_w': 8.0,
     'L2_gnn_gru_w_ih': 2.695,
     'L2_gnn_gru_b_ih': 3.723,
     'L2_gnn_gru_b_hh': 6.785}
    for name, (base, spread) in spreads.items():
        noise = np.random.default_rng([zlib.crc32(name.encode()), seed]).standard_normal(out[name].shape)
        drawn = base * np.exp(spread * noise) if base else spread * noise
        out[name] = jnp.asarray(drawn.astype(out[name].dtype))
    for name, factor in factors.items():
        out[name] = (out[name] * factor).astype(out[name].dtype)
    return out
```

```python
from contextlib import ExitStack

import concourse.bass as bass
from concourse import mybir

P = 128
N_NODES = 3125
NT = -(-N_NODES // P)
NP = NT * P
E = 100000
NC = -(-E // P)
EP = NC * P
PAD_DST = 4095
GT = 5
NG = NT // GT
GW = GT * P
HW = GW // 2
SPLIT = 3
BANK = 512
COPIES = 8

F32 = mybir.dt.float32
BF16 = mybir.dt.bfloat16
I32 = mybir.dt.int32
I16 = mybir.dt.int16
ALU = mybir.AluOpType
ACT = mybir.ActivationFunctionType
AX_X = mybir.AxisListType.X
ds = bass.ds
BIG = 1.0e30
ROUND = 8388608.0


def rows(ap, t, n=1):
    return ap[ds(t * P, n * P), :].rearrange("(n p) w -> p n w", p=P)


class Mem:

    phases = 0

    def __init__(self, nc, ctx):
        Mem.phases += 1
        self.nc, self.ctx, self.tag = nc, ctx, f"_{Mem.phases}"
        self.sems = []
        ctx.callback(self.clear)

    def sb(self, name, shape, dt=F32):
        return self.ctx.enter_context(self.nc.sbuf_tensor(name + self.tag, shape, dt))

    def ps(self, name, shape, dt=F32):
        return self.ctx.enter_context(self.nc.psum_tensor(name + self.tag, shape, dt))

    def sem(self, name):
        self.sems.append(self.nc.alloc_semaphore(name + self.tag))
        return self.sems[-1]

    def clear(self):
        if self.sems:
            self.nc.all_engine_barrier()
            self.nc.clear_and_free_semaphores(self.sems)
            self.nc.all_engine_barrier()



def make_constants(nc, K, D):
    with ExitStack() as ctx:
        m = Mem(nc, ctx)
        dst = m.sb("a_dst", [P, NC], I32)
        dstf = m.sb("a_dstf", [P, NC])
        junk = m.sb("a_junk", [P, NC])
        below = m.sb("a_below", [P, NT + 1])
        ones = m.sb("a_ones", [P, 1])
        row = m.sb("a_row", [1, NT + 1])
        rowi = m.sb("a_rowi", [1, NT + 1], I32)
        tiles = m.sb("a_tiles", [1, NT + 1])
        pcount = m.ps("a_pcount", [P, NT + 1])
        loaded, ready, counted, summed = (m.sem(f"a_{n}") for n in ("loaded", "ready", "counted", "summed"))
        with nc.Block() as block:
            @block.sync
            def _(sp):
                sp.dma_start(dst[:, :], D["dst_pc"]).then_inc(loaded, 16)

            @block.gpsimd
            def _(pool):
                pool.memset(K["identf"][:, :], 0.0).then_inc(ready, 1)
                pool.iota(tiles[:, :], pattern=[[1, NT + 1]], base=0, channel_multiplier=0,
                          allow_small_or_imprecise_dtypes=True).then_inc(ready, 1)
                pool.wait_ge(ready, 2)
                pool.affine_select(out=K["identf"][:, :], in_=K["identf"][:, :], compare_op=ALU.not_equal,
                                   fill=1.0, base=0, pattern=[[-1, P]], channel_multiplier=1).then_inc(ready, 1)

            @block.vector
            def _(dve):
                dve.memset(ones[:, :], 1.0)
                dve.memset(below[:, :], 0.0)
                dve.wait_ge(loaded, 16)
                dve.tensor_copy(dstf[:, :], dst[:, :])
                dve.drain()
                for t in range(1, NT + 1):
                    dve.tensor_scalar(junk[:, :], dstf[:, :], float(t * P), 0.0, ALU.is_lt, ALU.add,
                                      accum_out=below[:, t:t + 1])
                    dve.drain()
                dve.sem_inc(counted, 1)
                dve.wait_ge(ready, 3)
                dve.tensor_copy(K["identb"][:, :], K["identf"][:, :])
                dve.wait_ge(summed, 1)
                dve.tensor_copy(K["first_edge"][:, :], pcount[0:1, :])
                dve.drain()
                dve.tensor_copy(rowi[:, :], K["first_edge"][:, :])
                dve.drain()
                dve.tensor_scalar(rowi[:, :], rowi[:, :], 7, None, ALU.arith_shift_right)
                dve.drain()
                dve.tensor_copy(row[:, :], rowi[:, :])
                dve.drain()
                dve.tensor_tensor(row[:, :], row[:, :], tiles[:, :], ALU.add)
                dve.drain()
                dve.tensor_copy(K["bounds"][:, :], row[:, :])
                dve.drain()

            @block.tensor
            def _(pe):
                pe.wait_ge(counted, 1)
                pe.matmul(pcount[0:1, :], ones[:, :], below[:, :], start=True, stop=True).then_inc(summed, 1)


def build_counts(nc, K, D):
    BK = -(-NP // BANK)
    with ExitStack() as ctx:
        m = Mem(nc, ctx)
        dst = m.sb("b_dst", [P, NC], I32)
        src = m.sb("b_src", [P, NC], I32)
        dstf = m.sb("b_dstf", [P, NC + 2 * NT])
        srcf = m.sb("b_srcf", [P, NC + 2 * NT])
        lane = m.sb("b_lane", [P, NP], I16)
        lanef = m.sb("b_lanef", [P, NP])
        pick_dst = m.sb("b_pick_dst", [P, 2, P], BF16)
        pick_src = m.sb("b_pick_src", [P, 2, NP], BF16)
        zeros = m.sb("b_zeros", [P, BANK], BF16)
        arow = m.sb("b_arow", [P, NP], BF16)
        acc = m.ps("b_acc", [P, BK * BANK])
        loaded, ready, picked, used, closed, moved, diag, stored = (
            m.sem(f"b_{n}") for n in ("loaded", "ready", "picked", "used", "closed", "moved", "diag", "stored"))
        width = [min(BANK, NP - j * BANK) for j in range(BK)]

        def bounds(eng, t):
            lo = eng.value_load(K["bounds"][0:1, ds(t, 1)], min_val=0, max_val=NC + NT)
            hi = eng.value_load(K["bounds"][0:1, ds(t + 1, 1)], min_val=1, max_val=NC + NT)
            return lo, hi

        with nc.Block() as block:
            @block.sync
            def _(sp):
                sp.dma_start(dst[:, :], D["dst_pc"]).then_inc(loaded, 16)
                sp.dma_start(src[:, :], D["src_pc"]).then_inc(loaded, 16)
                with sp.Fori(0, NT) as t:
                    sp.wait_ge(diag, t + 1)
                    sp.dma_start(D["counts"][ds(t * P, P), :], arow[:, :]).then_inc(stored, 16)
                sp.wait_ge(stored, 16 * (NT + 1))

            @block.gpsimd
            def _(pool):
                pool.iota(lanef[:, :], pattern=[[1, NP]], base=0, channel_multiplier=0,
                          allow_small_or_imprecise_dtypes=True).then_inc(ready, 1)

            @block.vector
            def _(dve):
                dve.memset(zeros[:, :], 0.0)
                dve.drain().then_inc(used, 2)
                dve.wait_ge(ready, 1)
                dve.tensor_copy(lane[:, :], lanef[:, :])
                dve.wait_ge(loaded, 32)
                dve.tensor_copy(dstf[:, NT:NT + NC], dst[:, :])
                dve.tensor_copy(srcf[:, NT:NT + NC], src[:, :])
                dve.drain().then_inc(ready, 1)
                with dve.Fori(0, NT) as t:
                    lo, hi = bounds(dve, t)
                    with dve.Fori(lo, hi) as n:
                        c = n - t + NT
                        b = n % 2
                        dve.wait_ge(used, n + 1)
                        dve.tensor_scalar(pick_dst[:, ds(b, 1), :], lane[:, ds(t * P, P)],
                                          dstf[:, ds(c, 1)], None, ALU.is_equal)
                        dve.tensor_scalar(pick_src[:, ds(b, 1), :], lane[:, :],
                                          srcf[:, ds(c, 1)], None, ALU.is_equal).then_inc(picked, 1)
                    dve.wait_ge(moved, (t + 1) * BK + 1)
                    block_ = arow[:, ds(t * P, P)]
                    dve.tensor_tensor(block_, block_, K["identb"][:, :], ALU.add).then_inc(diag, 1)

            @block.scalar
            def _(act):
                act.sem_inc(moved, 1)
                act.sem_inc(stored, 16)
                with act.Fori(0, NT) as t:
                    act.wait_ge(closed, t + 1)
                    act.wait_ge(stored, 16 * (t + 1))
                    for j in range(BK):
                        act.activation(arow[:, j * BANK:j * BANK + width[j]],
                                       acc[:, j * BANK:j * BANK + width[j]], ACT.Copy).then_inc(moved, 1)

            @block.tensor
            def _(pe):
                pe.wait_ge(ready, 2)
                with pe.Fori(0, NT) as t:
                    lo, hi = bounds(pe, t)
                    pe.wait_ge(moved, t * BK + 1)
                    for j in range(BK):
                        pe.matmul(acc[:, j * BANK:j * BANK + width[j]], zeros[:, 0:P], zeros[:, 0:width[j]],
                                  start=True, stop=False, skip_group_check=True)
                    with pe.Fori(lo, hi) as n:
                        b = n % 2
                        pe.wait_ge(picked, n + 1)
                        for j in range(BK):
                            mm = pe.matmul(acc[:, j * BANK:j * BANK + width[j]], pick_dst[:, ds(b, 1), :],
                                           pick_src[:, ds(b, 1), j * BANK:j * BANK + width[j]],
                                           start=False, stop=False, skip_group_check=True)
                        mm.then_inc(used, 1)
                    for j in range(BK):
                        mm = pe.matmul(acc[:, j * BANK:j * BANK + width[j]], zeros[:, 0:P], zeros[:, 0:width[j]],
                                       start=False, stop=True, skip_group_check=True)
                    mm.then_inc(closed, 1)


def load_counts(nc, K, D, AT, outdeg=None):
    RB = 5
    with ExitStack() as ctx:
        m = Mem(nc, ctx)
        arows = m.sb("c_arows", [P, GT, NP], BF16)
        turned = [m.ps(f"c_turned{u}", [P, RB, P], BF16) for u in range(5)]
        ones = m.sb("c_ones", [P, 2], BF16)
        zeros = m.sb("c_zeros", [P, P], BF16)
        pdeg = m.ps("c_pdeg", [P, NT])
        loaded = [m.sem(f"c_loaded{u}") for u in range(GT)]
        ready, turned_in, act_out, dve_out, free = (m.sem(f"c_{n}") for n in ("ready", "turned", "act_out", "dve_out", "free"))
        with nc.Block() as block:
            @block.sync
            def _(sp):
                with sp.Fori(0, NG) as g:
                    for u in range(GT):
                        sp.wait_ge(free, g * GT + u + 1)
                        sp.dma_start(arows[:, u, :], D["counts"][ds((g * GT + u) * P, P), :]).then_inc(loaded[u], 16)

            @block.tensor
            def _(pe):
                pe.wait_ge(ready, 1)
                if outdeg is not None:
                    pe.matmul(pdeg[:, :], zeros[:, :], zeros[:, 0:NT], start=True, stop=False, skip_group_check=True)
                with pe.Fori(0, NG) as g:
                    for u in range(GT):
                        pe.wait_ge(loaded[u], g * 16 + 16)
                        for r in range(5):
                            if r % 2 == 0:
                                pe.wait_ge(act_out, (g * GT + u) * 3 + r // 2 + 1)
                            else:
                                pe.wait_ge(dve_out, (g * GT + u) * 2 + r // 2 + 1)
                            for i in range(RB):
                                j = r * RB + i
                                mm = pe.transpose(turned[r][:, i, :], arows[:, u, j * P:(j + 1) * P], K["identb"][:, :])
                            mm.then_inc(turned_in, 1)
                        if outdeg is not None:
                            for j in range(NT):
                                mm = pe.matmul(pdeg[:, j:j + 1], arows[:, u, j * P:(j + 1) * P], ones[:, 0:1],
                                               start=False, stop=False, skip_group_check=True)
                        pe.matmul(pdeg[:, 0:1], zeros[:, :], zeros[:, 0:1], start=outdeg is None, stop=outdeg is None,
                                  skip_group_check=True).then_inc(free, 1)
                if outdeg is not None:
                    pe.matmul(pdeg[:, :], zeros[:, :], zeros[:, 0:NT], start=False, stop=True,
                              skip_group_check=True).then_inc(ready, 1)

            def move(eng, copy, first, out, per):
                with eng.Fori(0, NG) as g:
                    for u in range(GT):
                        for r in range(first, 5, 2):
                            eng.wait_ge(turned_in, (g * GT + u) * 5 + r + 1)
                            copy(AT[:, r * RB:(r + 1) * RB, ds((g * GT + u) * P, P)], turned[r][:, :, :]).then_inc(out, 1)

            @block.scalar
            def _(act):
                act.sem_inc(act_out, 3)
                move(act, lambda o, i: act.activation(o, i, ACT.Copy), 0, act_out, 3)

            @block.vector
            def _(dve):
                dve.memset(zeros[:, :], 0.0)
                dve.memset(ones[:, :], 1.0)
                dve.drain().then_inc(ready, 1)
                dve.sem_inc(free, GT)
                dve.sem_inc(dve_out, 2)
                move(dve, lambda o, i: dve.tensor_copy(o, i), 1, dve_out, 2)
                if outdeg is not None:
                    dve.wait_ge(ready, 2)
                    dve.tensor_scalar(outdeg[:, :], pdeg[:, :], -1.0, None, ALU.add)
                    dve.drain()


def split_rows(nc, source, width, parts, scale=None):
    with ExitStack() as ctx:
        m = Mem(nc, ctx)
        NB = 2 if width <= P else 1
        stage = m.sb("s_stage", [P, NB, GT, width])
        loaded = [m.sem(f"s_loaded{b}") for b in range(NB)]
        hi, rest, mid, rest2, lo = (m.sem(f"s_{n}") for n in ("hi", "rest", "mid", "rest2", "lo"))
        with nc.Block() as block:
            @block.sync
            def _(sp):
                for g in range(NG):
                    if g >= NB:
                        sp.wait_ge(lo, g - NB + 1)
                    sp.dma_start(stage[:, g % NB, :, :], rows(source, g * GT, GT)).then_inc(loaded[g % NB], 16)

            @block.scalar
            def _(act):
                for g in range(NG):
                    part = [parts[:, k, g * GT:(g + 1) * GT, :] for k in range(SPLIT)]
                    if scale is None:
                        act.wait_ge(loaded[g % NB], 16 * (g // NB + 1))
                    else:
                        act.wait_ge(rest, 2 * g + 1)
                    act.activation(part[0], stage[:, g % NB, :, :], ACT.Copy).then_inc(hi, 1)
                    act.wait_ge(rest, 2 * g + 2)
                    act.activation(part[1], stage[:, g % NB, :, :], ACT.Copy).then_inc(mid, 1)
                    act.wait_ge(rest2, g + 1)
                    act.activation(part[2], stage[:, g % NB, :, :], ACT.Copy).then_inc(lo, 1)

            @block.vector
            def _(dve):
                for g in range(NG):
                    part = [parts[:, k, g * GT:(g + 1) * GT, :] for k in range(SPLIT)]
                    s = stage[:, g % NB, :, :]
                    if scale is not None:
                        dve.wait_ge(loaded[g % NB], 16 * (g // NB + 1))
                        dve.tensor_tensor(s, s, scale[:, g * GT:(g + 1) * GT].unsqueeze(2).broadcast_to([P, GT, width]),
                                          ALU.mult).then_inc(rest, 1)
                    else:
                        dve.sem_inc(rest, 1)
                    dve.wait_ge(hi, g + 1)
                    dve.tensor_tensor(s, s, part[0], ALU.subtract).then_inc(rest, 1)
                    dve.wait_ge(mid, g + 1)
                    dve.tensor_tensor(s, s, part[1], ALU.subtract).then_inc(rest2, 1)


def sum_neighbours(pe, AT, parts, banks, f, g, half):
    for j in range(NT):
        for k in range(SPLIT):
            mm = pe.matmul(banks, parts[:, k, j, f * P:(f + 1) * P], AT[:, j, ds(g * GW + half * HW, HW)],
                           start=(j == 0 and k == 0), stop=(j == NT - 1 and k == SPLIT - 1))
    return mm


def norm_stats(dve, y, stats, mv, n):
    for u in range(n):
        dve.bn_stats(stats[:, u, :], y[:, u, :])
    dve.drain()
    for u in range(n):
        dve.bn_aggr(mv[:, u, :], stats[:, u, :])
    dve.drain()
    dve.tensor_scalar(mv[:, 0:n, 1], mv[:, 0:n, 1], 1e-5, None, ALU.add)
    return dve.drain()


def norm_apply(dve, y, mv, n):
    dve.reciprocal(mv[:, 0:n, 1], mv[:, 0:n, 1])
    dve.drain()
    for u in range(n):
        dve.tensor_scalar(y[:, u, :], y[:, u, :], mv[:, u, 0:1], mv[:, u, 1:2], ALU.subtract, ALU.mult)
    return dve.drain()


def gin_conv(nc, K, D, AT, tag, source, fb, w1, b1, w2, b2, ow, target, residual):
    with ExitStack() as ctx:
        m = Mem(nc, ctx)
        parts = m.sb(f"{tag}_parts", [P, SPLIT, NT, fb * P], BF16)
        split_rows(nc, source, fb * P, parts)
        w1s = m.sb(f"{tag}_w1", [P, fb, 2 * P])
        w2s = m.sb(f"{tag}_w2", [P, 2, ow])
        b1s = m.sb(f"{tag}_b1", [P, 2])
        b2s = m.sb(f"{tag}_b2", [P, ow])
        hid = m.sb(f"{tag}_hid", [P, 2, GW])
        y = m.sb(f"{tag}_y", [P, GT, ow])
        stats = m.sb(f"{tag}_stats", [P, GT, 6])
        mv = m.sb(f"{tag}_mv", [P, GT, 2])
        pa = [m.ps(f"{tag}_pa{i}", [P, BANK]) for i in range(4)]
        pb = [m.ps(f"{tag}_pb{i}", [P, BANK]) for i in range(4)]
        weights, resid, summed, sums_out, hidden, hidden_out, made, taken, var, dev, done, stored = (
            m.sem(f"{tag}_{n}") for n in ("weights", "resid", "summed", "sums_out", "hidden", "hidden_out", "made",
                                          "taken", "var", "dev", "done", "stored"))
        NS = 2 * fb
        with nc.Block() as block:
            @block.sync
            def _(sp):
                sp.sem_inc(stored, 16)
                sp.dma_start(w1s[:, :, :], w1.rearrange("(k p) n -> p k n", p=P)).then_inc(weights, 16)
                sp.dma_start(w2s[:, :, :], w2.rearrange("(k p) n -> p k n", p=P)).then_inc(weights, 16)
                sp.dma_start(b1s[:, :], b1).then_inc(weights, 16)
                sp.dma_start(b2s[:, :], b2.partition_broadcast(P)).then_inc(weights, 16)
                with sp.Fori(0, NG) as g:
                    if residual is not None:
                        sp.wait_ge(stored, g * 16 + 16)
                        sp.dma_start(y[:, :, :], rows(residual, g * GT, GT)).then_inc(resid, 16)
                    sp.wait_ge(done, g + 1)
                    sp.dma_start(rows(target, g * GT, GT), y[:, :, :]).then_inc(stored, 16)
                sp.wait_ge(stored, 16 * NG + 16)

            @block.tensor
            def _(pe):
                pe.wait_ge(weights, 64)
                with pe.Fori(0, NG) as g:
                    pe.wait_ge(taken, g * GT + 1)
                    for f in range(fb):
                        for half in range(2):
                            sum_neighbours(pe, AT, parts, pa[2 * f + half][:, 0:HW], f, g, half).then_inc(summed, 1)
                    pe.wait_ge(sums_out, NS * (g + 1))
                    for o in range(2):
                        for half in range(2):
                            for k in range(fb):
                                mm = pe.matmul(pb[2 * o + half][:, 0:HW], w1s[:, k, o * P:(o + 1) * P],
                                               hid[:, k, half * HW:(half + 1) * HW], start=(k == 0), stop=(k == fb - 1))
                    mm.then_inc(hidden, 1)
                    pe.wait_ge(hidden_out, 4 * (g + 1))
                    for u in range(GT):
                        if u == 4:
                            pe.wait_ge(taken, g * GT + 2)
                        for k in range(2):
                            mm = pe.matmul(pa[u % 4][:, 0:ow], hid[:, k, u * P:(u + 1) * P], w2s[:, k, :],
                                           start=(k == 0), stop=(k == 1))
                        mm.then_inc(made, 1)

            @block.scalar
            def _(act):
                act.wait_ge(weights, 64)
                with act.Fori(0, NG) as g:
                    act.wait_ge(hidden, g + 1)
                    for o in range(2):
                        for half in range(2):
                            act.activation(hid[:, o, half * HW:(half + 1) * HW], pb[2 * o + half][:, 0:HW], ACT.Relu,
                                           bias=b1s[:, o:o + 1]).then_inc(hidden_out, 1)
                    if residual is not None:
                        act.wait_ge(var, g + 1)
                        act.activation(mv[:, :, 1], mv[:, :, 1], ACT.Sqrt).then_inc(dev, 1)

            @block.vector
            def _(dve):
                dve.sem_inc(taken, 1)
                dve.wait_ge(weights, 64)
                with dve.Fori(0, NG) as g:
                    if residual is not None:
                        dve.wait_ge(resid, g * 16 + 16)
                        dve.tensor_tensor(y[:, :, :], y[:, :, :], b2s[:, :].unsqueeze(1).broadcast_to([P, GT, ow]), ALU.add)
                    for f in range(fb):
                        for half in range(2):
                            dve.wait_ge(summed, g * NS + 2 * f + half + 1)
                            dve.tensor_copy(hid[:, f, half * HW:(half + 1) * HW], pa[2 * f + half][:, 0:HW]).then_inc(sums_out, 1)
                    dve.drain()
                    if residual is None:
                        dve.wait_ge(stored, g * 16 + 16)
                    for u in range(GT):
                        dve.wait_ge(made, g * GT + u + 1)
                        dve.tensor_tensor(y[:, u, :], pa[u % 4][:, 0:ow], b2s[:, :] if residual is None else y[:, u, :],
                                          ALU.add).then_inc(taken, 1)
                    dve.drain()
                    if residual is None:
                        dve.tensor_scalar(y[:, :, :], y[:, :, :], 0.0, None, ALU.max).then_inc(done, 1)
                    else:
                        norm_stats(dve, y, stats, mv, GT).then_inc(var, 1)
                        dve.wait_ge(dev, g + 1)
                        norm_apply(dve, y, mv, GT).then_inc(done, 1)


HEADS = 4
PAIRS = HEADS // 2
SC = 400
SR = 2 * SC
ROUNDS = NP // SR
TB = 4
TR = -(-NT // TB)
FAR = 3.0e38


def attention(nc, K, D, source, fin, w, att_l, att_r, bias, ch, target, elu):
    FB = fin // P
    wd = HEADS * ch
    HB = wd // P
    per = P // ch
    with ExitStack() as ctx:
        m = Mem(nc, ctx)
        xwt = m.sb("t_xwt", [P, HB, NP])
        xw = m.sb("t_xw", [P, NT, HEADS, ch + 1])
        al = m.sb("t_al", [P, HEADS, NP])
        ar = m.sb("t_ar", [P, NT, HEADS])
        biasb = m.sb("t_bias", [P, wd])

        with ExitStack() as ctx2:
            m2 = Mem(nc, ctx2)
            ws = m2.sb("t_w", [P, FB, wd])
            attl = m2.sb("t_attl", [P, HB])
            attlb = m2.sb("t_attlb", [P, HB, P])
            attr = m2.sb("t_attr", [P, HB, per])
            x = m2.sb("t_x", [P, GT, fin])
            xt = m2.sb("t_xt", [P, FB, GW])
            ptr = [m2.ps(f"t_ptr{i}", [P, BANK]) for i in range(2)]
            pxt = [m2.ps(f"t_pxt{i}", [P, BANK]) for i in range(2)]
            pxw = [m2.ps(f"t_pxw{i}", [P, BANK]) for i in range(2)]
            par = m2.ps("t_par", [P, NT, HEADS])
            weights, loaded, turned, xt_out, free, xwt_made, xwt_out, xw_made, xw_out, al_made, al_out, ones_in, ar_made = (
                m2.sem(f"t_{n}") for n in ("weights", "loaded", "turned", "xt_out", "free", "xwt_made", "xwt_out",
                                           "xw_made", "xw_out", "al_made", "al_out", "ones_in", "ar_made"))
            NTURN = FB * 2
            with nc.Block() as block:
                @block.sync
                def _(sp):
                    sp.dma_start(ws[:, :, :], w.rearrange("(k p) n -> p k n", p=P)).then_inc(weights, 16)
                    sp.dma_start(attl[:, :], att_l).then_inc(weights, 16)
                    sp.dma_start(attr[:, :, :], att_r).then_inc(weights, 16)
                    sp.dma_start(biasb[:, :], bias.partition_broadcast(P)).then_inc(weights, 16)
                    with sp.Fori(0, NG) as g:
                        sp.wait_ge(turned, g * GT * FB + 1)
                        sp.dma_start(x[:, :, :], rows(source, g * GT, GT)).then_inc(loaded, 16)

                @block.tensor
                def _(pe):
                    pe.sem_inc(xw_made, 1)
                    pe.sem_inc(turned, 1)
                    pe.wait_ge(weights, 64)
                    with pe.Fori(0, NG) as g:
                        pe.wait_ge(loaded, g * 16 + 16)
                        for u in range(GT):
                            for k in range(FB):
                                i = u * FB + k
                                pe.wait_ge(xt_out, g * GT * FB + i + 1)
                                pe.transpose(ptr[i % 2][:, 0:P], x[:, u, k * P:(k + 1) * P], K["identf"][:, :]).then_inc(turned, 1)
                        pe.wait_ge(xt_out, (g + 1) * GT * FB + 2)
                        for hb in range(HB):
                            for half in range(2):
                                i = hb * 2 + half
                                pe.wait_ge(xwt_out, g * 2 * HB + i + 1)
                                for k in range(FB):
                                    mm = pe.matmul(pxt[i % 2][:, 0:HW], ws[:, k, hb * P:(hb + 1) * P],
                                                   xt[:, k, half * HW:(half + 1) * HW], start=(k == 0), stop=(k == FB - 1))
                                mm.then_inc(xwt_made, 1)
                        for u in range(GT):
                            pe.wait_ge(xw_out, g * GT + u + 1)
                            for k in range(FB):
                                mm = pe.matmul(pxw[u % 2][:, 0:wd], xt[:, k, u * P:(u + 1) * P], ws[:, k, :],
                                               start=(k == 0), stop=(k == FB - 1))
                            mm.then_inc(xw_made, 1)
                    pe.wait_ge(xwt_out, NG * 2 * HB + 2)
                    pe.wait_ge(xw_out, NG * GT + 2)
                    pe.wait_ge(ones_in, 1)
                    for h in range(HEADS):
                        hb, off = h // per, (h % per) * ch
                        for t in range(NT):
                            mm = pe.matmul(par[:, t, h:h + 1], xwt[:, hb, t * P:(t + 1) * P],
                                           attr[:, hb, h % per:h % per + 1], start=True, stop=True)
                        for q in range(NP // SC):
                            i = h * (NP // SC) + q
                            if i >= 2:
                                pe.wait_ge(al_out, i - 1)
                            pe.matmul(pxt[i % 2][:, 0:SC], attlb[off:off + ch, hb, :],
                                      xwt[off:off + ch, hb, q * SC:(q + 1) * SC], start=True, stop=True).then_inc(al_made, 1)
                    mm.then_inc(ar_made, 1)

                @block.scalar
                def _(act):
                    act.sem_inc(xwt_out, 2)
                    with act.Fori(0, NG) as g:
                        for hb in range(HB):
                            for half in range(2):
                                i = hb * 2 + half
                                act.wait_ge(xwt_made, g * 2 * HB + i + 1)
                                act.activation(xwt[:, hb, ds(g * GW + half * HW, HW)], pxt[i % 2][:, 0:HW],
                                               ACT.Copy).then_inc(xwt_out, 1)
                    for i in range(HEADS * NP // SC):
                        h, q = divmod(i, NP // SC)
                        act.wait_ge(al_made, i + 1)
                        act.activation(al[:, h, q * SC:(q + 1) * SC], pxt[i % 2][:, 0:SC], ACT.Copy).then_inc(al_out, 1)

                @block.vector
                def _(dve):
                    dve.sem_inc(xt_out, 2)
                    dve.sem_inc(xw_out, 2)
                    dve.memset(xw[:, :, :, ch:ch + 1], 1.0)
                    dve.wait_ge(weights, 64)
                    dve.tensor_copy(attlb[:, :, :], attl[:, :].unsqueeze(2).broadcast_to([P, HB, P]))
                    dve.drain().then_inc(ones_in, 1)
                    with dve.Fori(0, NG) as g:
                        for u in range(GT):
                            for k in range(FB):
                                i = u * FB + k
                                dve.wait_ge(turned, g * GT * FB + i + 2)
                                if i == 0:
                                    dve.wait_ge(xw_made, g * GT + 1)
                                dve.tensor_copy(xt[:, k, u * P:(u + 1) * P], ptr[i % 2][:, 0:P]).then_inc(xt_out, 1)
                        for u in range(GT):
                            dve.wait_ge(xw_made, g * GT + u + 2)
                            dve.tensor_copy(xw[:, ds(g * GT + u, 1), :, 0:ch],
                                            pxw[u % 2][:, 0:wd].rearrange("p (o h c) -> p o h c", o=1, h=HEADS)).then_inc(xw_out, 1)
                    dve.wait_ge(ar_made, 1)
                    dve.tensor_copy(ar[:, :, :], par[:, :, :])
                    dve.drain()

        counts = m.sb("t_counts", [P, 2, NP], BF16)
        absent = m.sb("t_absent", [P, NP], BF16)
        panel = [m.sb(f"t_panel{h}", [P, NP]) for h in range(HEADS)]
        panel_t = m.sb("t_panel_t", [P, NT, P])
        query = m.sb("t_query", [P, HB, P])
        top = m.sb("t_top", [P, HEADS, 2])
        inv = m.sb("t_inv", [P, HEADS])
        out = m.sb("t_out", [P, wd])
        neg = m.sb("t_neg", [P, wd])
        ps = [m.ps(f"t_ps{i}", [P, 2, BANK]) for i in range(2)]
        pt = [m.ps(f"t_pt{i}", [P, BANK]) for i in range(2)]
        po = [m.ps(f"t_po{i}", [P, BANK]) for i in range(2)]
        (loaded, query_in, scored, sigmoid, maxed, exps, weighted, turned, turned_out, applied, taken,
         low, low_exp, done, stored, pool_passed, sp_passed) = (
            m.sem(f"t_{n}") for n in ("loaded", "query_in", "scored", "sigmoid", "maxed", "exps",
                                      "weighted", "turned", "turned_out", "applied", "taken", "low", "low_exp", "done",
                                      "stored", "pool_passed", "sp_passed"))

        def heads(t, pair):
            return [(h, t * HEADS + h) for h in (2 * pair, 2 * pair + 1)]

        def stages(eng, score, weigh, take, finish):
            score(0, 0)
            score(0, 1)
            weigh(0, 0)
            with eng.Fori(0, NT - 1) as t:
                score(t + 1, 0)
                take(t, 0)
                weigh(t, 1)
                score(t + 1, 1)
                take(t, 1)
                finish(t)
                weigh(t + 1, 0)
            take(NT - 1, 0)
            weigh(NT - 1, 1)
            take(NT - 1, 1)
            finish(NT - 1)

        def nothing(*_):
            return None

        with nc.Block() as block:
            @block.sync
            def _(sp):
                sp.sem_inc(loaded, 16)
                def load(t):
                    slot, row = sp.snap(t % 2), sp.snap(t * P)
                    sp.wait_ge(weighted, t * HEADS + 1)
                    sp.sem_inc(sp_passed, 1)
                    sp.wait_ge(loaded, t * 16 + 16)
                    sp.sem_inc(sp_passed, 1)
                    sp.dma_start(counts[:, ds(slot, 1), :],
                                 D["counts"][ds(row, P), :].rearrange("p (o s) -> p o s", o=1)).then_inc(loaded, 16)

                def store(t):
                    sp.wait_ge(done, t + 1)
                    sp.dma_start(target[ds(t * P, P), :], out[:, :]).then_inc(stored, 16)
                load(0)
                with sp.Fori(0, NT - 1) as t:
                    load(t + 1)
                    store(t)
                store(NT - 1)
                sp.wait_ge(stored, 16 * (NT + 1))

            @block.gpsimd
            def _(pool):
                def score(t, pair):
                    if pair == 0:
                        pool.wait_ge(scored, t * HEADS * ROUNDS + 1)
                        pool.tensor_copy(query[:, :, :], xwt[:, :, ds(t * P, P)]).then_inc(query_in, 1)

                def weigh(t, pair):
                    for h, n in heads(t, pair):
                        pool.wait_ge(exps, n + 1)
                        pool.sem_inc(pool_passed, 1)
                        pool.tensor_tensor(panel[h][:, :], panel[h][:, :],
                                           counts[:, ds(t % 2, 1), :].rearrange("p o s -> p (o s)"), ALU.mult).then_inc(weighted, 1)
                stages(pool, score, weigh, nothing, nothing)

            @block.tensor
            def _(pe):
                pe.sem_inc(applied, 1)
                pe.sem_inc(scored, 1)
                def score(t, pair):
                    if pair == 0:
                        pe.wait_ge(query_in, t + 1)
                    for h, n in heads(t, pair):
                        hb, off = h // per, (h % per) * ch
                        for r in range(ROUNDS):
                            pe.wait_ge(sigmoid, n * ROUNDS + r + 1)
                            for i in range(2):
                                c = r * SR + i * SC
                                mm = pe.matmul(ps[r % 2][:, i, 0:SC], query[off:off + ch, hb, :],
                                               xwt[off:off + ch, hb, c:c + SC], start=True, stop=True)
                            mm.then_inc(scored, 1)

                def weigh(t, pair):
                    for h, n in heads(t, pair):
                        pe.wait_ge(weighted, n + HEADS + 2)
                        for r in range(TR):
                            pe.wait_ge(turned_out, n * TR + r + 1)
                            for i in range(min(TB, NT - r * TB)):
                                j = r * TB + i
                                mm = pe.transpose(pt[r % 2][:, i * P:(i + 1) * P], panel[h][:, j * P:(j + 1) * P],
                                                  K["identf"][:, :])
                            mm.then_inc(turned, 1)
                        pe.wait_ge(turned_out, n * TR + TR + 2)
                        pe.wait_ge(taken, n + 1)
                        for j in range(NT):
                            mm = pe.matmul(po[h % 2][:, 0:ch + 1], panel_t[:, j, :], xw[:, j, h, :],
                                           start=(j == 0), stop=(j == NT - 1))
                        mm.then_inc(applied, 1)
                stages(pe, score, weigh, nothing, nothing)

            @block.scalar
            def _(act):
                act.sem_inc(sigmoid, 2)
                act.sem_inc(turned_out, 2)

                def score(t, pair):
                    for h, n in heads(t, pair):
                        act.wait_ge(turned, n * TR + 1)
                        for r in range(ROUNDS):
                            act.wait_ge(scored, n * ROUNDS + r + 2)
                            act.activation(panel[h][:, r * SR:(r + 1) * SR].rearrange("p (i c) -> p i c", i=2),
                                           ps[r % 2][:, :, 0:SC], ACT.Sigmoid).then_inc(sigmoid, 1)

                def weigh(t, pair):
                    for h, n in heads(t, pair):
                        act.wait_ge(maxed, n + 1)
                        act.activation(panel[h][:, :], panel[h][:, :], ACT.Exp, bias=top[:, h, 1:2]).then_inc(exps, 1)
                    for h, n in heads(t, pair):
                        act.wait_ge(applied, n + 1)
                        for r in range(TR):
                            b = min(TB, NT - r * TB)
                            act.wait_ge(turned, (n + HEADS - 1) * TR + r + 2)
                            act.activation(panel_t[:, r * TB:r * TB + b, :],
                                           pt[r % 2][:, 0:b * P].rearrange("p (b d) -> p b d", b=b), ACT.Copy).then_inc(turned_out, 1)

                def finish(t):
                    if elu:
                        act.wait_ge(low, t + 1)
                        act.activation(neg[:, :], neg[:, :], ACT.Exp).then_inc(low_exp, 1)
                stages(act, score, weigh, nothing, finish)

            @block.vector
            def _(dve):
                dve.sem_inc(weighted, HEADS + 1)
                dve.sem_inc(turned, (HEADS - 1) * TR + 1)
                dve.sem_inc(taken, 2)
                dve.sem_inc(stored, 16)

                def score(t, pair):
                    if pair == 0:
                        dve.wait_ge(loaded, t * 16 + 32)
                        dve.tensor_scalar(absent[:, :], counts[:, ds(t % 2, 1), :].rearrange("p o s -> p (o s)"),
                                          0.0, -BIG, ALU.is_equal, ALU.mult)
                    for h, n in heads(t, pair):
                        dve.wait_ge(sigmoid, n * ROUNDS + ROUNDS + 2)
                        dve.scalar_tensor_tensor(out=panel[h][:, :], in0=al[:, h, :],
                                                 scalar=ar[:, ds(t, 1), h:h + 1].rearrange("p o h -> p (o h)"),
                                                 in1=panel[h][:, :], op0=ALU.add, op1=ALU.mult)
                        dve.drain()
                        dve.tensor_tensor_reduce(panel[h][:, :], panel[h][:, :], absent[:, :], 1.0, -FAR, ALU.add, ALU.max,
                                                 top[:, h, 0:1])
                        dve.drain()
                        dve.scalar_tensor_tensor(out=panel[h][:, :], in0=panel[h][:, :], scalar=0.2, in1=panel[h][:, :],
                                                 op0=ALU.mult, op1=ALU.max)
                        dve.scalar_tensor_tensor(out=top[:, h, 1:2], in0=top[:, h, 0:1], scalar=0.2, in1=top[:, h, 0:1],
                                                 op0=ALU.mult, op1=ALU.max)
                        dve.drain()
                        dve.tensor_scalar(top[:, h, 1:2], top[:, h, 1:2], -1.0, None, ALU.mult).then_inc(maxed, 1)

                def take(t, pair):
                    if pair == 0:
                        dve.wait_ge(stored, t * 16 + 16)
                    for h, n in heads(t, pair):
                        dve.wait_ge(applied, n + 2)
                        dve.tensor_scalar(inv[:, h:h + 1], po[h % 2][:, ch:ch + 1], 1e-16, None, ALU.add)
                        dve.drain()
                        dve.reciprocal(inv[:, h:h + 1], inv[:, h:h + 1])
                        dve.drain()
                        dve.scalar_tensor_tensor(out=out[:, h * ch:(h + 1) * ch], in0=po[h % 2][:, 0:ch],
                                                 scalar=inv[:, h:h + 1], in1=biasb[:, h * ch:(h + 1) * ch],
                                                 op0=ALU.mult, op1=ALU.add).then_inc(taken, 1)

                def finish(t):
                    dve.drain()
                    if elu:
                        dve.tensor_scalar(neg[:, :], out[:, :], 0.0, None, ALU.min).then_inc(low, 1)
                        dve.drain()
                        dve.tensor_scalar(out[:, :], out[:, :], 0.0, None, ALU.max)
                        dve.drain()
                        dve.wait_ge(low_exp, t + 1)
                        dve.scalar_tensor_tensor(out=out[:, :], in0=neg[:, :], scalar=-1.0, in1=out[:, :],
                                                 op0=ALU.add, op1=ALU.add)
                        dve.drain()
                    dve.sem_inc(done, 1)
                stages(dve, score, nothing, take, finish)


def softmax_norm(nc, K, source, residual, target):
    with ExitStack() as ctx:
        m = Mem(nc, ctx)
        v = m.sb("u_v", [P, NT, P])
        x = m.sb("u_x", [P, NT, P])
        e = m.sb("u_e", [P, NT, P])
        top = m.sb("u_top", [P, NT])
        total = m.sb("u_total", [P, NT])
        stats = m.sb("u_stats", [P, NT, 6])
        mv = m.sb("u_mv", [P, NT, 2])
        loaded, step, act_step, stored = (m.sem(f"u_{n}") for n in ("loaded", "step", "act_step", "stored"))
        wide = [P, NT, P]
        with nc.Block() as block:
            @block.sync
            def _(sp):
                sp.dma_start(v[:, :, :], source.rearrange("(t p) f -> p t f", p=P)).then_inc(loaded, 16)
                sp.dma_start(x[:, :, :], residual.rearrange("(t p) f -> p t f", p=P)).then_inc(loaded, 16)
                sp.wait_ge(step, 4)
                sp.dma_start(target.rearrange("(t p) f -> p t f", p=P), x[:, :, :]).then_inc(stored, 16)
                sp.wait_ge(stored, 16)

            @block.scalar
            def _(act):
                act.wait_ge(step, 1)
                act.activation(e[:, :, :], v[:, :, :], ACT.Exp).then_inc(act_step, 1)
                act.wait_ge(step, 2)
                act.activation(total[:, :], total[:, :], ACT.Ln).then_inc(act_step, 1)
                act.wait_ge(step, 3)
                act.activation(mv[:, :, 1], mv[:, :, 1], ACT.Sqrt).then_inc(act_step, 1)

            @block.vector
            def _(dve):
                dve.wait_ge(loaded, 32)
                dve.tensor_reduce(top[:, :], v[:, :, :], AX_X, ALU.max)
                dve.drain()
                dve.tensor_tensor(v[:, :, :], v[:, :, :], top[:, :].unsqueeze(2).broadcast_to(wide), ALU.subtract)
                dve.drain().then_inc(step, 1)
                dve.tensor_tensor(x[:, :, :], x[:, :, :], v[:, :, :], ALU.add)
                dve.wait_ge(act_step, 1)
                dve.tensor_reduce(total[:, :], e[:, :, :], AX_X, ALU.add)
                dve.drain().then_inc(step, 1)
                dve.wait_ge(act_step, 2)
                dve.tensor_tensor(x[:, :, :], x[:, :, :], total[:, :].unsqueeze(2).broadcast_to(wide), ALU.subtract)
                dve.drain()
                norm_stats(dve, x, stats, mv, NT).then_inc(step, 1)
                dve.wait_ge(act_step, 3)
                norm_apply(dve, x, mv, NT).then_inc(step, 1)


GATES = 3


def gru_degrees(nc, K, AT, outdeg, from_scale, to_scale):
    Q = NP // SC
    with ExitStack() as ctx:
        m = Mem(nc, ctx)
        ones = m.sb("d_ones", [P, P], BF16)
        psum = [m.ps(f"d_psum{i}", [P, BANK]) for i in range(2)]
        ready, made, moved, clipped, rooted = (m.sem(f"d_{n}") for n in ("ready", "made", "moved", "clipped", "rooted"))
        with nc.Block() as block:
            @block.vector
            def _(dve):
                dve.memset(ones[:, :], 1.0)
                for t in range(NT):
                    block_ = AT[:, t, t * P:(t + 1) * P]
                    dve.tensor_tensor(block_, block_, K["identb"][:, :], ALU.subtract)
                dve.drain().then_inc(ready, 1)
                dve.tensor_scalar(from_scale[:, :], outdeg[:, :], 1.0, None, ALU.max)
                for q in range(Q):
                    dve.wait_ge(made, q + 1)
                    dve.tensor_scalar(to_scale[:, q * SC:(q + 1) * SC], psum[q % 2][:, 0:SC], 1.0, None, ALU.max).then_inc(moved, 1)
                dve.drain().then_inc(clipped, 1)
                dve.wait_ge(rooted, 2)
                dve.reciprocal(from_scale[:, :], from_scale[:, :])
                dve.reciprocal(to_scale[:, :], to_scale[:, :])
                dve.drain()

            @block.scalar
            def _(act):
                act.wait_ge(clipped, 1)
                act.activation(from_scale[:, :], from_scale[:, :], ACT.Sqrt).then_inc(rooted, 1)
                act.activation(to_scale[:, :], to_scale[:, :], ACT.Sqrt).then_inc(rooted, 1)

            @block.tensor
            def _(pe):
                pe.wait_ge(ready, 1)
                for q in range(Q):
                    if q >= 2:
                        pe.wait_ge(moved, q - 1)
                    for j in range(NT):
                        mm = pe.matmul(psum[q % 2][:, 0:SC], ones[:, :], AT[:, j, q * SC:(q + 1) * SC],
                                       start=(j == 0), stop=(j == NT - 1))
                    mm.then_inc(made, 1)


def gru_block(nc, K, D, AT, b, source, from_scale, to_scale, parts, target, residual):
    split_rows(nc, source, P, parts, from_scale)
    with ExitStack() as ctx:
        m = Mem(nc, ctx)
        wg = m.sb("r_wg", [P, P])
        wi = m.sb("r_wi", [P, GATES * P])
        bg = m.sb("r_bg", [P, 1])
        bi = m.sb("r_bi", [P, GATES])
        bh = m.sb("r_bh", [P, GATES])
        brz = m.sb("r_brz", [P, 2])
        summed = m.sb("r_summed", [P, GW])
        conv = m.sb("r_conv", [P, GW])
        reset = m.sb("r_reset", [P, GW])
        keep = m.sb("r_keep", [P, GW])
        cand = m.sb("r_cand", [P, GW])
        y = m.sb("r_y", [P, GT, P])
        stats = m.sb("r_stats", [P, GT, 6])
        mv = m.sb("r_mv", [P, GT, 2])
        pa = [m.ps(f"r_pa{i}", [P, BANK]) for i in range(2)]
        pg = [[m.ps(f"r_pg{c}{i}", [P, BANK]) for i in range(2)] for c in range(GATES)]
        (weights, biases, sums, sums_out, convs, convs_out, gates, gates_out, mixed, tanned, state, turned, taken,
         resid, var, dev, done, stored) = (
            m.sem(f"r_{n}") for n in ("weights", "biases", "sums", "sums_out", "convs", "convs_out", "gates",
                                      "gates_out", "mixed", "tanned", "state", "turned", "taken", "resid", "var", "dev",
                                      "done", "stored"))
        halves = [slice(i * HW, (i + 1) * HW) for i in range(2)]
        with nc.Block() as block:
            @block.sync
            def _(sp):
                sp.sem_inc(stored, 16)
                sp.dma_start(wg[:, :], D["gcn_w"][b * P:(b + 1) * P, :]).then_inc(weights, 16)
                sp.dma_start(wi[:, :], D["gru_w"][b * P:(b + 1) * P, :]).then_inc(weights, 16)
                sp.dma_start(bg[:, :], D["gcn_b"][b * P:(b + 1) * P, :]).then_inc(weights, 16)
                sp.dma_start(bi[:, :], D["gru_bi"][b * P:(b + 1) * P, :]).then_inc(weights, 16)
                sp.dma_start(bh[:, :], D["gru_bh"][b * P:(b + 1) * P, :]).then_inc(weights, 16)
                with sp.Fori(0, NG) as g:
                    if residual is not None:
                        sp.wait_ge(stored, g * 16 + 16)
                        sp.dma_start(y[:, :, :], rows(residual, g * GT, GT)).then_inc(resid, 16)
                    sp.wait_ge(done, g + 1)
                    sp.dma_start(rows(target, g * GT, GT), y[:, :, :]).then_inc(stored, 16)
                sp.wait_ge(stored, 16 * NG + 16)

            @block.tensor
            def _(pe):
                pe.sem_inc(turned, 1)
                pe.wait_ge(weights, 80)
                with pe.Fori(0, NG) as g:
                    pe.wait_ge(taken, g * GT + 1)
                    for i in range(2):
                        sum_neighbours(pe, AT, parts, pa[i][:, 0:HW], 0, g, i).then_inc(sums, 1)
                    for i in range(2):
                        pe.wait_ge(sums_out, g * 2 + i + 1)
                        pe.matmul(pg[2][i][:, 0:HW], wg[:, :], summed[:, halves[i]], start=True, stop=True).then_inc(convs, 1)
                    pe.wait_ge(convs_out, g * 2 + 2)
                    for c in range(GATES):
                        for i in range(2):
                            pe.matmul(pg[c][i][:, 0:HW], wi[:, c * P:(c + 1) * P], conv[:, halves[i]],
                                      start=True, stop=True).then_inc(gates, 1)
                    pe.wait_ge(state, g + 1)
                    for u in range(GT):
                        pe.transpose(pa[u // 4][:, u % 4 * P:(u % 4 + 1) * P], cand[:, u * P:(u + 1) * P],
                                     K["identf"][:, :]).then_inc(turned, 1)

            @block.scalar
            def _(act):
                act.wait_ge(biases, 1)
                with act.Fori(0, NG) as g:
                    for i in range(2):
                        act.wait_ge(convs, g * 2 + i + 1)
                        act.activation(conv[:, halves[i]], pg[2][i][:, 0:HW], ACT.Identity, bias=bg[:, 0:1]).then_inc(convs_out, 1)
                    for i in range(2):
                        act.wait_ge(gates, g * 6 + i + 1)
                        act.activation(reset[:, halves[i]], pg[0][i][:, 0:HW], ACT.Sigmoid, bias=brz[:, 0:1]).then_inc(gates_out, 1)
                    for i in range(2):
                        act.wait_ge(gates, g * 6 + 3 + i)
                        act.activation(keep[:, halves[i]], pg[1][i][:, 0:HW], ACT.Sigmoid, bias=brz[:, 1:2], scale=-1.0).then_inc(gates_out, 1)
                    act.wait_ge(mixed, g * 2 + 2)
                    act.activation(cand[:, :], cand[:, :], ACT.Tanh, bias=bi[:, 2:3]).then_inc(tanned, 1)
                    if residual is not None:
                        act.wait_ge(var, g + 1)
                        act.activation(mv[:, :, 1], mv[:, :, 1], ACT.Sqrt).then_inc(dev, 1)

            @block.vector
            def _(dve):
                dve.sem_inc(taken, 1)
                dve.wait_ge(weights, 80)
                dve.tensor_tensor(brz[:, :], bi[:, 0:2], bh[:, 0:2], ALU.add)
                dve.drain()
                dve.tensor_scalar(brz[:, 1:2], brz[:, 1:2], -1.0, None, ALU.mult)
                dve.drain().then_inc(biases, 1)
                with dve.Fori(0, NG) as g:
                    for i in range(2):
                        dve.wait_ge(sums, g * 2 + i + 1)
                        dve.tensor_tensor(summed[:, halves[i]], pa[i][:, 0:HW], to_scale[:, ds(g * GW + i * HW, HW)],
                                          ALU.mult).then_inc(sums_out, 1)
                    dve.drain()
                    dve.wait_ge(turned, g * GT + 1)
                    for i in range(2):
                        dve.wait_ge(gates_out, g * 4 + i + 1)
                        dve.wait_ge(gates, g * 6 + 5 + i)
                        dve.scalar_tensor_tensor(out=cand[:, halves[i]], in0=reset[:, halves[i]], scalar=bh[:, 2:3],
                                                 in1=pg[2][i][:, 0:HW], op0=ALU.mult, op1=ALU.add).then_inc(mixed, 1)
                    dve.wait_ge(gates_out, g * 4 + 4)
                    dve.wait_ge(tanned, g + 1)
                    dve.scalar_tensor_tensor(out=cand[:, :], in0=cand[:, :], scalar=0.0, in1=keep[:, :],
                                             op0=ALU.max, op1=ALU.mult).then_inc(state, 1)
                    if residual is None:
                        dve.wait_ge(stored, g * 16 + 16)
                    else:
                        dve.wait_ge(resid, g * 16 + 16)
                    for u in range(GT):
                        if u in (0, 4):
                            dve.wait_ge(turned, g * GT + min(u + 4, GT) + 1)
                        result = pa[u // 4][:, u % 4 * P:(u % 4 + 1) * P]
                        if residual is None:
                            dve.tensor_copy(y[:, u, :], result).then_inc(taken, 1)
                        else:
                            dve.tensor_tensor(y[:, u, :], result, y[:, u, :], ALU.add).then_inc(taken, 1)
                    if residual is not None:
                        dve.drain()
                        norm_stats(dve, y, stats, mv, GT).then_inc(var, 1)
                        dve.wait_ge(dev, g + 1)
                        norm_apply(dve, y, mv, GT)
                    dve.drain()
                    dve.sem_inc(done, 1)


RBF = 64
SUB = 4
STEPS = -(-NC // SUB)
NCS = STEPS * SUB


def edge_messages(nc, K, D, source):
    with ExitStack() as ctx:
        m = Mem(nc, ctx)
        W = SUB * P
        src = m.sb("e_src", [P, NCS], I32)
        dst = m.sb("e_dst", [P, NCS], I32)
        dump = m.sb("e_dump", [P, 1])
        before = m.sb("e_before", [P, P])
        zeros = m.sb("e_zeros", [P, NT + 1, P])
        w1 = m.sb("e_w1", [RBF, P])
        w2 = m.sb("e_w2", [P, P])
        b1 = m.sb("e_b1", [P, 1])
        b2 = m.sb("e_b2", [P, P])
        rbf = m.sb("e_rbf", [P, SUB, RBF])
        rbft = m.sb("e_rbft", [RBF, W])
        hid = m.sb("e_hid", [P, W])
        gate = m.sb("e_gate", [P, W])
        src_row = m.sb("e_src_row", [P, 2, W], I32)
        srcf = m.sb("e_srcf", [P, SUB])
        gap = m.sb("e_gap", [P, SUB])
        earlier = m.sb("e_earlier", [P, SUB])
        target = m.sb("e_target", [P, SUB], I32)
        near = m.sb("e_near", [P, SUB], I32)
        same = m.sb("e_same", [P, W])
        junk = m.sb("e_junk", [P, P])
        nodes = m.sb("e_nodes", [P, SUB, P])
        msg = m.sb("e_msg", [P, SUB, P])
        merged = m.sb("e_merged", [P, SUB, P])
        pt, ph, pw, pm = (m.ps(f"e_p{n}", [P, BANK]) for n in "thwm")
        tables, ready, zeroed, passed, sp_passed, pe_passed = (
            m.sem(f"e_{n}") for n in ("tables", "ready", "zeroed", "passed", "sp_passed", "pe_passed"))
        (edges, turned, turned_out, hids, gated, hid_out, filt, filt_out, nears, sames, targets, msgs, merges,
         merges_out) = (
            m.sem(f"e_{n}") for n in ("edges", "turned", "turned_out", "hids", "gated", "hid_out", "filt", "filt_out", "nears",
                                      "sames", "targets", "msgs", "merges", "merges_out"))
        gathered = [m.sem(f"e_gathered{u}") for u in range(SUB)]
        scattered = [m.sem(f"e_scattered{u}") for u in range(SUB)]
        with nc.Block() as block:
            @block.sync
            def _(sp):
                sp.sem_inc(edges, 16)
                sp.dma_start(src[:, :], D["src_pc2"]).then_inc(tables, 16)
                sp.dma_start(dst[:, :], D["dst_pc2"]).then_inc(tables, 16)
                sp.dma_start(w1[:, :], D["e_W1"]).then_inc(tables, 16)
                sp.dma_start(w2[:, :], D["e_W2"]).then_inc(tables, 16)
                sp.dma_start(b1[:, :], D["e_b1"]).then_inc(tables, 16)
                sp.dma_start(b2[:, :], D["e_b2"].partition_broadcast(P)).then_inc(tables, 16)
                with sp.Fori(0, STEPS) as i:
                    slot, row = sp.snap(i % 2), sp.snap(i * W)
                    sp.wait_ge(edges, i * 32 + 16)
                    sp.sem_inc(sp_passed, 1)
                    sp.wait_ge(turned, i + 1)
                    sp.wait_ge(sames, i + 1)
                    sp.sem_inc(sp_passed, 1)
                    sp.dma_start(rbf[:, :, :],
                                 D["edge_attr"][ds(row, W), :].rearrange("(u p) r -> p u r", p=P)).then_inc(edges, 16)
                    sp.dma_start(src_row[:, ds(slot, 1), :].rearrange("p o e -> p (o e)"),
                                 D["src_row"][0:1, ds(row, W)].broadcast_to([P, W])).then_inc(edges, 16)

            @block.gpsimd
            def _(pool):
                pool.iota(dump[:, :], pattern=[[0, 1]], base=NP, channel_multiplier=1,
                          allow_small_or_imprecise_dtypes=True).then_inc(ready, 1)
                pool.memset(before[:, :], 1.0).then_inc(ready, 1)
                pool.wait_ge(ready, 2)
                pool.affine_select(out=before[:, :], in_=before[:, :], compare_op=ALU.is_gt, fill=0.0, base=0,
                                   pattern=[[-1, P]], channel_multiplier=1).then_inc(ready, 1)
                pool.wait_ge(zeroed, 1)
                for u in range(SUB):
                    pool.dma_start(D["acc"][u].rearrange("(t p) f -> p t f", p=P), zeros[:, :, :]).then_inc(scattered[u], 16)

                def gather(i):
                    pool.wait_ge(nears, i + 1)
                    for u in range(SUB):
                        pool.wait_ge(msgs, i * SUB + u + 1)
                        pool.sem_inc(passed, 1)
                        pool.indirect_dma_start(out=nodes[:, u, :], out_offset=None, in_=source,
                                                in_offset=bass.IndirectOffsetOnAxis(ap=near[:, u:u + 1], axis=0)).then_inc(gathered[u], 16)

                def scatter(i):
                    pool.wait_ge(targets, i + 1)
                    for u in range(SUB):
                        pool.wait_ge(merges_out, i * SUB + u + 2)
                        pool.wait_ge(scattered[u], i * 16 + 16)
                        pool.sem_inc(passed, 1)
                        pool.indirect_dma_start(out=D["acc"][u], in_=merged[:, u, :], in_offset=None, compute_op=ALU.add,
                                                out_offset=bass.IndirectOffsetOnAxis(ap=target[:, u:u + 1], axis=0)).then_inc(scattered[u], 16)
                gather(0)
                with pool.Fori(0, STEPS - 1) as i:
                    gather(i + 1)
                    scatter(i)
                scatter(STEPS - 1)
                for u in range(SUB):
                    pool.wait_ge(scattered[u], 16 * STEPS + 16)

            @block.tensor
            def _(pe):
                pe.sem_inc(turned, 1)
                pe.sem_inc(hids, 1)
                pe.sem_inc(filt, 1)
                pe.sem_inc(merges, 1)
                pe.wait_ge(tables, 96)
                with pe.Fori(0, STEPS) as i:
                    pe.wait_ge(edges, i * 32 + 48)
                    pe.wait_ge(turned_out, i + 1)
                    pe.sem_inc(pe_passed, 1)
                    for u in range(SUB):
                        mm = pe.transpose(pt[0:RBF, u * P:(u + 1) * P],
                                          rbf[:, u, :], K["identf"][:, :])
                    mm.then_inc(turned, 1)
                    pe.wait_ge(turned_out, i + 2)
                    pe.wait_ge(hid_out, i + 1)
                    pe.matmul(ph[:, :], w1[:, :], rbft[:, :], start=True, stop=True).then_inc(hids, 1)
                    pe.wait_ge(hid_out, i + 2)
                    pe.wait_ge(filt_out, i + 1)
                    for u in range(SUB):
                        mm = pe.matmul(pw[:, u * P:(u + 1) * P], hid[:, u * P:(u + 1) * P], w2[:, :], start=True, stop=True)
                    mm.then_inc(filt, 1)
                    pe.wait_ge(sames, i + 2)
                    pe.wait_ge(merges_out, i * SUB + 1)
                    for u in range(SUB):
                        pe.wait_ge(msgs, (i + 1) * SUB + u + 1)
                        pe.matmul(pm[:, u * P:(u + 1) * P], same[:, u * P:(u + 1) * P], msg[:, u, :],
                                  start=True, stop=True).then_inc(merges, 1)

            @block.scalar
            def _(act):
                act.sem_inc(turned_out, 1)
                act.sem_inc(hid_out, 1)
                act.sem_inc(merges_out, 1)
                act.wait_ge(tables, 96)
                with act.Fori(0, STEPS) as i:
                    act.wait_ge(hids, i + 1)
                    act.wait_ge(turned, i + 2)
                    act.activation(rbft[:, :], pt[0:RBF, :], ACT.Copy).then_inc(turned_out, 1)
                    act.wait_ge(filt, i + 1)
                    act.wait_ge(hids, i + 2)
                    act.activation(hid[:, :], ph[:, :], ACT.Silu, bias=b1[:, 0:1]).then_inc(hid_out, 1)
                    for u in range(SUB):
                        act.wait_ge(merges, (i + 1) * SUB + 1)
                        act.wait_ge(scattered[u], i * 16 + 16)
                        act.activation(merged[:, u, :], pm[:, u * P:(u + 1) * P], ACT.Copy).then_inc(merges_out, 1)

            @block.vector
            def _(dve):
                dve.sem_inc(sames, 1)
                dve.sem_inc(filt_out, 1)
                dve.memset(zeros[:, :, :], 0.0).then_inc(zeroed, 1)
                dve.sem_inc(msgs, SUB)
                dve.wait_ge(tables, 96)
                dve.tensor_scalar(dst[:, :], dst[:, :], float(NP - 1), None, ALU.min)
                dve.drain()

                def near_of(i):
                    dve.tensor_copy(near[:, :], dst[:, ds(i * SUB, SUB)]).then_inc(nears, 1)
                near_of(0)
                dve.wait_ge(ready, 3)

                def step(i):
                    dve.tensor_copy(srcf[:, :], src[:, ds(i * SUB, SUB)])
                    dve.drain()
                    dve.tensor_scalar(gap[:, :], srcf[:, :], dump[:, 0:1], -1.0, ALU.subtract, ALU.mult)
                    dve.wait_ge(edges, i * 32 + 48)
                    dve.wait_ge(merges, i * SUB + 1)
                    for u in range(SUB):
                        dve.tensor_scalar(same[:, u * P:(u + 1) * P],
                                          src_row[:, ds(i % 2, 1), u * P:(u + 1) * P].rearrange("p o e -> p (o e)"),
                                          srcf[:, u:u + 1], None, ALU.is_equal)
                    dve.drain().then_inc(sames, 1)
                    for u in range(SUB):
                        dve.tensor_tensor_reduce(junk[:, :], same[:, u * P:(u + 1) * P], before[:, :], 1.0, 0.0,
                                                 ALU.mult, ALU.add, earlier[:, u:u + 1])
                        dve.drain()
                    dve.scalar_tensor_tensor(out=gap[:, :], in0=earlier[:, :], scalar=0.0, in1=gap[:, :],
                                             op0=ALU.is_gt, op1=ALU.mult)
                    dve.drain()
                    for u in range(SUB):
                        dve.wait_ge(scattered[u], i * 16 + 16)
                    dve.tensor_tensor(target[:, :], gap[:, :], srcf[:, :], ALU.add).then_inc(targets, 1)
                    dve.wait_ge(filt, i + 2)
                    dve.tensor_tensor(msg[:, :, :], pw[:, :].rearrange("p (u f) -> p u f", u=SUB),
                                      b2[:, :].unsqueeze(1).broadcast_to([P, SUB, P]), ALU.add).then_inc(filt_out, 1)
                    dve.drain()
                    for u in range(SUB):
                        dve.wait_ge(gathered[u], i * 16 + 16)
                        dve.tensor_tensor(msg[:, u, :], msg[:, u, :], nodes[:, u, :], ALU.mult).then_inc(msgs, 1)

                with dve.Fori(0, STEPS - 1) as i:
                    dve.wait_ge(gathered[SUB - 1], i * 16 + 16)
                    for u in range(SUB - 1):
                        dve.wait_ge(gathered[u], i * 16 + 16)
                    near_of(i + 1)
                    step(i)
                step(STEPS - 1)


def node_update(nc, K, D, source, target):
    with ExitStack() as ctx:
        m = Mem(nc, ctx)
        w3 = m.sb("n_w3", [P, P])
        w4 = m.sb("n_w4", [P, P])
        b3 = m.sb("n_b3", [P, 1])
        b4 = m.sb("n_b4", [P, P])
        part = m.sb("n_part", [P, SUB, GT, P])
        x = m.sb("n_x", [P, GT, P])
        aggt = m.sb("n_aggt", [P, GW])
        hid = m.sb("n_hid", [P, GW])
        stats = m.sb("n_stats", [P, GT, 6])
        mv = m.sb("n_mv", [P, GT, 2])
        pt = [m.ps(f"n_pt{i}", [P, BANK]) for i in range(2)]
        ph = [m.ps(f"n_ph{i}", [P, BANK]) for i in range(2)]
        po = [m.ps(f"n_po{i}", [P, BANK]) for i in range(2)]
        weights, loaded, x_loaded, added, turned, turned_out, hids, hid_out, outs, var, dev, done, stored, sp_passed = (
            m.sem(f"n_{n}") for n in ("weights", "loaded", "x_loaded", "added", "turned", "turned_out", "hids", "hid_out", "outs",
                                      "var", "dev", "done", "stored", "sp_passed"))
        with nc.Block() as block:
            @block.sync
            def _(sp):
                sp.sem_inc(stored, 16)
                sp.dma_start(w3[:, :], D["e_W3"]).then_inc(weights, 16)
                sp.dma_start(w4[:, :], D["e_W4"]).then_inc(weights, 16)
                sp.dma_start(b3[:, :], D["e_b3"]).then_inc(weights, 16)
                sp.dma_start(b4[:, :], D["e_b4"].partition_broadcast(P)).then_inc(weights, 16)
                with sp.Fori(0, NG) as g:
                    sp.wait_ge(stored, g * 16 + 16)
                    for u in range(SUB):
                        sp.dma_start(part[:, u, :, :], rows(D["acc"][u], g * GT, GT)).then_inc(loaded, 16)
                    sp.dma_start(x[:, :, :], rows(source, g * GT, GT)).then_inc(x_loaded, 16)
                    sp.wait_ge(x_loaded, g * 16 + 16)
                    sp.sem_inc(sp_passed, 1)
                    sp.wait_ge(done, g + 1)
                    sp.dma_start(rows(target, g * GT, GT), x[:, :, :]).then_inc(stored, 16)
                sp.wait_ge(stored, 16 * NG + 16)

            @block.tensor
            def _(pe):
                pe.wait_ge(weights, 64)
                with pe.Fori(0, NG) as g:
                    pe.wait_ge(added, g + 1)
                    for u in range(GT):
                        mm = pe.transpose(pt[u // 4][:, u % 4 * P:(u % 4 + 1) * P], part[:, 0, u, :], K["identf"][:, :])
                    mm.then_inc(turned, 1)
                    pe.wait_ge(turned_out, g + 1)
                    for i in range(2):
                        pe.matmul(ph[i][:, 0:HW], w3[:, :], aggt[:, i * HW:(i + 1) * HW], start=True, stop=True).then_inc(hids, 1)
                    pe.wait_ge(hid_out, g * 2 + 2)
                    for u in range(GT):
                        mm = pe.matmul(po[u // 4][:, u % 4 * P:(u % 4 + 1) * P], hid[:, u * P:(u + 1) * P], w4[:, :],
                                       start=True, stop=True)
                    mm.then_inc(outs, 1)

            @block.scalar
            def _(act):
                act.wait_ge(weights, 64)
                with act.Fori(0, NG) as g:
                    for i in range(2):
                        act.wait_ge(hids, g * 2 + i + 1)
                        act.activation(hid[:, i * HW:(i + 1) * HW], ph[i][:, 0:HW], ACT.Silu, bias=b3[:, 0:1]).then_inc(hid_out, 1)
                    act.wait_ge(var, g + 1)
                    act.activation(mv[:, :, 1], mv[:, :, 1], ACT.Sqrt).then_inc(dev, 1)

            @block.vector
            def _(dve):
                dve.wait_ge(weights, 64)
                with dve.Fori(0, NG) as g:
                    dve.wait_ge(loaded, (g + 1) * SUB * 16)
                    for u in range(1, SUB):
                        dve.tensor_tensor(part[:, 0, :, :], part[:, 0, :, :], part[:, u, :, :], ALU.add)
                        dve.drain()
                    dve.sem_inc(added, 1)
                    dve.wait_ge(x_loaded, g * 16 + 16)
                    dve.tensor_scalar(x[:, :, :], x[:, :, :], 2.0, None, ALU.mult)
                    dve.drain()
                    dve.tensor_tensor(x[:, :, :], x[:, :, :], b4[:, :].unsqueeze(1).broadcast_to([P, GT, P]), ALU.add)
                    dve.wait_ge(turned, g + 1)
                    dve.tensor_copy(aggt[:, 0:4 * P], pt[0][:, :])
                    dve.tensor_copy(aggt[:, 4 * P:GW], pt[1][:, 0:P])
                    dve.drain().then_inc(turned_out, 1)
                    dve.wait_ge(outs, g + 1)
                    for u in range(GT):
                        dve.tensor_tensor(x[:, u, :], x[:, u, :], po[u // 4][:, u % 4 * P:(u % 4 + 1) * P], ALU.add)
                    dve.drain()
                    norm_stats(dve, x, stats, mv, GT).then_inc(var, 1)
                    dve.wait_ge(dev, g + 1)
                    norm_apply(dve, x, mv, GT).then_inc(done, 1)


LAYERS = 4


def gnn_program(nc, D):
    def scratch(name, shape, dt=F32):
        D[name] = nc.dram_tensor(name, shape, dt, kind="Internal").ap()

    scratch("counts", [NP, NP], BF16)
    for name in ("x1", "gat2", "x2", "x3"):
        scratch(name, [NP, P])
    for name in ("gin1", "gat1"):
        scratch(name, [NP, 2 * P])
    states = []
    for b in range(LAYERS - 1):
        scratch(f"state{b}", [NP, P])
        states.append(D[f"state{b}"])
    D["acc"] = [nc.dram_tensor(f"acc{u}", [NP + P, P], F32, kind="Internal").ap() for u in range(SUB)]

    with ExitStack() as ctx:
        m = Mem(nc, ctx)
        K = dict(identf=m.sb("identf", [P, P]), identb=m.sb("identb", [P, P], BF16),
                 bounds=m.sb("bounds", [1, NT + 1], I32), first_edge=m.sb("first_edge", [1, NT + 1]))
        make_constants(nc, K, D)
        build_counts(nc, K, D)
        with ExitStack() as ctx2:
            AT = Mem(nc, ctx2).sb("gin_counts", [P, NT, NP], BF16)
            load_counts(nc, K, D, AT)
            gin_conv(nc, K, D, AT, "g0", D["x"], 1, D["L0_W1a"], D["L0_b1a"], D["L0_W2a"], D["L0_b2a"], 2 * P,
                     D["gin1"], None)
            gin_conv(nc, K, D, AT, "g1", D["gin1"], 2, D["L0_W1b"], D["L0_b1b"], D["L0_W2b"], D["L0_b2b"], P,
                     D["x1"], D["x"])
        attention(nc, K, D, D["x1"], P, D["L1_W1"], D["L1_att_l1"], D["L1_att_r1"], D["L1_b1"], 2 * P // HEADS,
                  D["gat1"], True)
        attention(nc, K, D, D["gat1"], 2 * P, D["L1_W2"], D["L1_att_l2"], D["L1_att_r2"], D["L1_b2"], P // HEADS,
                  D["gat2"], False)
        softmax_norm(nc, K, D["gat2"], D["x1"], D["x2"])
        with ExitStack() as ctx2:
            m2 = Mem(nc, ctx2)
            outdeg = m2.sb("outdeg", [P, NT])
            AT = m2.sb("gru_counts", [P, NT, NP], BF16)
            load_counts(nc, K, D, AT, outdeg)
            to_scale = m2.sb("to_scale", [P, NP])
            from_scale = m2.sb("from_scale", [P, NT])
            parts = m2.sb("gru_parts", [P, SPLIT, NT, P], BF16)
            gru_degrees(nc, K, AT, outdeg, from_scale, to_scale)
            chain = [D["x2"], *states, D["x3"]]
            for b in range(LAYERS):
                gru_block(nc, K, D, AT, b, chain[b], from_scale, to_scale, parts, chain[b + 1],
                          D["x2"] if b == LAYERS - 1 else None)
        edge_messages(nc, K, D, D["x3"])
        node_update(nc, K, D, D["x3"], D["out"])


def laid_out(inputs):
    import numpy as np

    a = {n: np.asarray(v) for n, v in inputs.items()}

    def edges(v, fill, chunks):
        full = np.full(chunks * P, fill, v.dtype)
        full[:E] = v
        return full

    def by_chunk(v):
        return np.ascontiguousarray(v.reshape(-1, P).T)

    def padded(v, n):
        full = np.zeros((n, v.shape[1]), v.dtype)
        full[:v.shape[0]] = v
        return full

    def column(v):
        return np.ascontiguousarray(v.reshape(-1, P).T)

    def by_head(v):
        heads, ch = v.shape
        per = P // ch
        full = np.zeros((P, heads // per, per), v.dtype)
        for h in range(heads):
            full[h % per * ch:(h % per + 1) * ch, h // per, h % per] = v[h]
        return full

    src, dst = edges(a["src"], NP - 1, NCS), edges(a["dst"], PAD_DST, NCS)
    out = {
        "x": padded(a["x"], NP),
        "dst_pc": by_chunk(dst[:EP]), "src_pc": by_chunk(src[:EP]),
        "dst_pc2": by_chunk(dst), "src_pc2": by_chunk(src), "src_row": src.reshape(1, -1),
        "edge_attr": padded(a["edge_attr_64"], NCS * P),
    }
    for n in ("W1a", "W2a", "b2a", "W1b", "W2b", "b2b"):
        out[f"L0_{n}"] = a[f"L0_gnn_{n}"]
    for n in ("b1a", "b1b"):
        out[f"L0_{n}"] = column(a[f"L0_gnn_{n}"])
    for n in ("W1", "W2", "b1", "b2"):
        out[f"L1_{n}"] = a[f"L1_gnn_{n}"]
    for n in ("1", "2"):
        out[f"L1_att_l{n}"] = column(a[f"L1_gnn_att_l{n}"])
        out[f"L1_att_r{n}"] = by_head(a[f"L1_gnn_att_r{n}"])
    out["gcn_w"] = a["L2_gnn_gcn_w"].reshape(LAYERS * P, P)
    out["gcn_b"] = a["L2_gnn_gcn_b"].reshape(LAYERS * P, 1)
    out["gru_w"] = np.ascontiguousarray(a["L2_gnn_gru_w_ih"].transpose(0, 2, 1)).reshape(LAYERS * P, GATES * P)
    for n, name in (("gru_bi", "b_ih"), ("gru_bh", "b_hh")):
        v = a[f"L2_gnn_gru_{name}"].reshape(LAYERS, GATES, P)
        out[n] = np.ascontiguousarray(v.transpose(0, 2, 1)).reshape(LAYERS * P, GATES)
    for n in ("W1", "W2", "W3", "W4", "b2", "b4"):
        out[f"e_{n}"] = a[f"L3_gnn_{n}"]
    for n in ("b1", "b3"):
        out[f"e_{n}"] = a[f"L3_gnn_{n}"].reshape(P, 1)
    return {n: np.ascontiguousarray(v) for n, v in out.items()}


def kernel(**inputs):
    import concourse.bacc as bacc
    from concourse.bass_utils import run_bass_kernel_spmd

    nc = bacc.Bacc("TRN2", target_bir_lowering=False, num_devices=1)
    arrays, D = {}, {}
    for name, v in laid_out(inputs).items():
        arrays[f"in_{name}"] = v
        D[name] = nc.dram_tensor(f"in_{name}", list(v.shape), mybir.dt.from_np(v.dtype), kind="ExternalInput").ap()
    D["out"] = nc.dram_tensor("out", [NP, P], F32, kind="ExternalOutput").ap()
    gnn_program(nc, D)
    r = run_bass_kernel_spmd(nc, [arrays], core_ids=[0])
    return r.results[0]["out"][:N_NODES]
```

```python
from contextlib import ExitStack

import concourse.bass as bass
from concourse import mybir

P = 128
N_NODES = 3125
NT = -(-N_NODES // P)
NP = NT * P
E = 100000
STEP = 2 * P
NC = -(-E // STEP) * 2
EP = NC * P
PAD_DST = 4095
GT = 5
NG = NT // GT
STEP_BITS = 8
assert STEP == 1 << STEP_BITS
GW = GT * P
HW = GW // 2
SPLIT = 3
BANK = 512
COPIES = 8

F32 = mybir.dt.float32
BF16 = mybir.dt.bfloat16
I32 = mybir.dt.int32
I16 = mybir.dt.int16
ALU = mybir.AluOpType
ACT = mybir.ActivationFunctionType
AX_X = mybir.AxisListType.X
ds = bass.ds
BIG = 1.0e30
ROUND = 8388608.0


def rows(ap, t, n=1):
    return ap[ds(t * P, n * P), :].rearrange("(n p) w -> p n w", p=P)


class Mem:

    phases = 0

    def __init__(self, nc, ctx):
        Mem.phases += 1
        self.nc, self.ctx, self.tag = nc, ctx, f"_{Mem.phases}"
        self.sems = []
        ctx.callback(self.clear)

    def sb(self, name, shape, dt=F32):
        return self.ctx.enter_context(self.nc.sbuf_tensor(name + self.tag, shape, dt))

    def ps(self, name, shape, dt=F32):
        return self.ctx.enter_context(self.nc.psum_tensor(name + self.tag, shape, dt))

    def sem(self, name):
        self.sems.append(self.nc.alloc_semaphore(name + self.tag))
        return self.sems[-1]

    def clear(self):
        if self.sems:
            self.nc.all_engine_barrier()
            self.nc.clear_and_free_semaphores(self.sems)
            self.nc.all_engine_barrier()



def make_constants(nc, K, D):
    with ExitStack() as ctx:
        m = Mem(nc, ctx)
        dst = m.sb("a_dst", [P, NC], I32)
        dstf = m.sb("a_dstf", [P, NC])
        junk = m.sb("a_junk", [P, NC])
        below = m.sb("a_below", [P, NT + 1])
        ones = m.sb("a_ones", [P, 1])
        row = m.sb("a_row", [1, NT + 1])
        rowi = m.sb("a_rowi", [1, NT + 1], I32)
        tiles = m.sb("a_tiles", [1, NT + 1])
        pcount = m.ps("a_pcount", [P, NT + 1])
        loaded, ready, counted, summed = (m.sem(f"a_{n}") for n in ("loaded", "ready", "counted", "summed"))
        with nc.Block() as block:
            @block.sync
            def _(sp):
                sp.dma_start(dst[:, :], D["dst_pc"]).then_inc(loaded, 16)

            @block.gpsimd
            def _(pool):
                pool.memset(K["identf"][:, :], 0.0).then_inc(ready, 1)
                pool.iota(tiles[:, :], pattern=[[1, NT + 1]], base=0, channel_multiplier=0,
                          allow_small_or_imprecise_dtypes=True).then_inc(ready, 1)
                pool.wait_ge(ready, 2)
                pool.affine_select(out=K["identf"][:, :], in_=K["identf"][:, :], compare_op=ALU.not_equal,
                                   fill=1.0, base=0, pattern=[[-1, P]], channel_multiplier=1).then_inc(ready, 1)

            @block.vector
            def _(dve):
                dve.memset(ones[:, :], 1.0)
                dve.memset(below[:, :], 0.0)
                dve.wait_ge(loaded, 16)
                dve.tensor_copy(dstf[:, :], dst[:, :])
                dve.drain()
                for t in range(1, NT + 1):
                    dve.tensor_scalar(junk[:, :], dstf[:, :], float(t * P), 0.0, ALU.is_lt, ALU.add,
                                      accum_out=below[:, t:t + 1])
                    dve.drain()
                dve.sem_inc(counted, 1)
                dve.wait_ge(ready, 3)
                dve.tensor_copy(K["identb"][:, :], K["identf"][:, :])
                dve.wait_ge(summed, 1)
                dve.tensor_copy(K["first_edge"][:, :], pcount[0:1, :])
                dve.drain()
                dve.tensor_copy(rowi[:, :], K["first_edge"][:, :])
                dve.drain()
                dve.tensor_scalar(rowi[:, :], rowi[:, :], STEP_BITS, None, ALU.arith_shift_right)
                dve.drain()
                dve.tensor_copy(row[:, :], rowi[:, :])
                dve.drain()
                dve.tensor_tensor(row[:, :], row[:, :], tiles[:, :], ALU.add)
                dve.drain()
                dve.tensor_copy(K["bounds"][:, :], row[:, :])
                dve.drain()

            @block.tensor
            def _(pe):
                pe.wait_ge(counted, 1)
                pe.matmul(pcount[0:1, :], ones[:, :], below[:, :], start=True, stop=True).then_inc(summed, 1)


def build_counts(nc, K, D):
    BK = -(-NP // BANK)
    with ExitStack() as ctx:
        m = Mem(nc, ctx)
        dst = m.sb("b_dst", [P, NC], I32)
        src = m.sb("b_src", [P, NC], I32)
        dstf = m.sb("b_dstf", [P, NC + 4 * NT])
        srcf = m.sb("b_srcf", [P, NC + 4 * NT])
        lane = m.sb("b_lane", [P, NP], I16)
        lanef = m.sb("b_lanef", [P, NP])
        pick_dst = m.sb("b_pick_dst", [P, 2, P], BF16)
        pick_src = m.sb("b_pick_src", [P, 2, NP], BF16)
        zeros = m.sb("b_zeros", [P, BANK], BF16)
        arow = m.sb("b_arow", [P, NP], BF16)
        acc = m.ps("b_acc", [P, BK * BANK])
        loaded, ready, picked, used, closed, moved, diag, stored = (
            m.sem(f"b_{n}") for n in ("loaded", "ready", "picked", "used", "closed", "moved", "diag", "stored"))
        width = [min(BANK, NP - j * BANK) for j in range(BK)]

        def bounds(eng, t):
            lo = eng.value_load(K["bounds"][0:1, ds(t, 1)], min_val=0, max_val=NC // 2 + NT)
            hi = eng.value_load(K["bounds"][0:1, ds(t + 1, 1)], min_val=1, max_val=NC // 2 + NT)
            return lo, hi

        with nc.Block() as block:
            @block.sync
            def _(sp):
                sp.dma_start(dst[:, :], D["dst_pc"]).then_inc(loaded, 16)
                sp.dma_start(src[:, :], D["src_pc"]).then_inc(loaded, 16)
                with sp.Fori(0, NT) as t:
                    sp.wait_ge(diag, t + 1)
                    sp.dma_start(D["counts"][ds(t * P, P), :], arow[:, :]).then_inc(stored, 16)
                sp.wait_ge(stored, 16 * (NT + 1))

            @block.gpsimd
            def _(pool):
                pool.iota(lanef[:, :], pattern=[[1, NP]], base=0, channel_multiplier=0,
                          allow_small_or_imprecise_dtypes=True).then_inc(ready, 1)

            @block.vector
            def _(dve):
                dve.memset(zeros[:, :], 0.0)
                dve.drain().then_inc(used, 2)
                dve.wait_ge(ready, 1)
                dve.tensor_copy(lane[:, :], lanef[:, :])
                dve.wait_ge(loaded, 32)
                dve.tensor_copy(dstf[:, 2 * NT:2 * NT + NC], dst[:, :])
                dve.tensor_copy(srcf[:, 2 * NT:2 * NT + NC], src[:, :])
                dve.drain().then_inc(ready, 1)
                with dve.Fori(0, NT) as t:
                    lo, hi = bounds(dve, t)
                    with dve.Fori(lo, hi) as n:
                        for b in range(2):
                            c = dve.snap((n - t + NT) * 2 + b)
                            dve.wait_ge(used, n * 2 + b + 1)
                            dve.tensor_scalar(pick_dst[:, b, :], lane[:, ds(t * P, P)],
                                              dstf[:, ds(c, 1)], None, ALU.is_equal)
                            dve.tensor_scalar(pick_src[:, b, :], lane[:, :],
                                              srcf[:, ds(c, 1)], None, ALU.is_equal).then_inc(picked, 1)
                    dve.wait_ge(moved, (t + 1) * BK + 1)
                    block_ = arow[:, ds(t * P, P)]
                    dve.tensor_tensor(block_, block_, K["identb"][:, :], ALU.add).then_inc(diag, 1)

            @block.scalar
            def _(act):
                act.sem_inc(moved, 1)
                act.sem_inc(stored, 16)
                with act.Fori(0, NT) as t:
                    act.wait_ge(closed, t + 1)
                    act.wait_ge(stored, 16 * (t + 1))
                    for j in range(BK):
                        act.activation(arow[:, j * BANK:j * BANK + width[j]],
                                       acc[:, j * BANK:j * BANK + width[j]], ACT.Copy).then_inc(moved, 1)

            @block.tensor
            def _(pe):
                pe.wait_ge(ready, 2)
                with pe.Fori(0, NT) as t:
                    lo, hi = bounds(pe, t)
                    pe.wait_ge(moved, t * BK + 1)
                    for j in range(BK):
                        pe.matmul(acc[:, j * BANK:j * BANK + width[j]], zeros[:, 0:P], zeros[:, 0:width[j]],
                                  start=True, stop=False, skip_group_check=True)
                    with pe.Fori(lo, hi) as n:
                        for b in range(2):
                            pe.wait_ge(picked, n * 2 + b + 1)
                            for j in range(BK):
                                mm = pe.matmul(acc[:, j * BANK:j * BANK + width[j]], pick_dst[:, b, :],
                                               pick_src[:, b, j * BANK:j * BANK + width[j]],
                                               start=False, stop=False, skip_group_check=True)
                            mm.then_inc(used, 1)
                    for j in range(BK):
                        mm = pe.matmul(acc[:, j * BANK:j * BANK + width[j]], zeros[:, 0:P], zeros[:, 0:width[j]],
                                       start=False, stop=True, skip_group_check=True)
                    mm.then_inc(closed, 1)


def load_counts(nc, K, D, AT, outdeg=None):
    RB = 5
    with ExitStack() as ctx:
        m = Mem(nc, ctx)
        arows = m.sb("c_arows", [P, GT, NP], BF16)
        turned = [m.ps(f"c_turned{u}", [P, RB, P], BF16) for u in range(5)]
        ones = m.sb("c_ones", [P, 2], BF16)
        zeros = m.sb("c_zeros", [P, P], BF16)
        pdeg = m.ps("c_pdeg", [P, NT])
        loaded = [m.sem(f"c_loaded{u}") for u in range(GT)]
        ready, turned_in, act_out, dve_out, free = (m.sem(f"c_{n}") for n in ("ready", "turned", "act_out", "dve_out", "free"))
        with nc.Block() as block:
            @block.sync
            def _(sp):
                with sp.Fori(0, NG) as g:
                    for u in range(GT):
                        sp.wait_ge(free, g * GT + u + 1)
                        sp.dma_start(arows[:, u, :], D["counts"][ds((g * GT + u) * P, P), :]).then_inc(loaded[u], 16)

            @block.tensor
            def _(pe):
                pe.wait_ge(ready, 1)
                if outdeg is not None:
                    pe.matmul(pdeg[:, :], zeros[:, :], zeros[:, 0:NT], start=True, stop=False, skip_group_check=True)
                with pe.Fori(0, NG) as g:
                    for u in range(GT):
                        pe.wait_ge(loaded[u], g * 16 + 16)
                        for r in range(5):
                            if r % 2 == 0:
                                pe.wait_ge(act_out, (g * GT + u) * 3 + r // 2 + 1)
                            else:
                                pe.wait_ge(dve_out, (g * GT + u) * 2 + r // 2 + 1)
                            for i in range(RB):
                                j = r * RB + i
                                mm = pe.transpose(turned[r][:, i, :], arows[:, u, j * P:(j + 1) * P], K["identb"][:, :])
                            mm.then_inc(turned_in, 1)
                        if outdeg is not None:
                            for j in range(NT):
                                mm = pe.matmul(pdeg[:, j:j + 1], arows[:, u, j * P:(j + 1) * P], ones[:, 0:1],
                                               start=False, stop=False, skip_group_check=True)
                        pe.matmul(pdeg[:, 0:1], zeros[:, :], zeros[:, 0:1], start=outdeg is None, stop=outdeg is None,
                                  skip_group_check=True).then_inc(free, 1)
                if outdeg is not None:
                    pe.matmul(pdeg[:, :], zeros[:, :], zeros[:, 0:NT], start=False, stop=True,
                              skip_group_check=True).then_inc(ready, 1)

            def move(eng, copy, first, out, per):
                with eng.Fori(0, NG) as g:
                    for u in range(GT):
                        for r in range(first, 5, 2):
                            eng.wait_ge(turned_in, (g * GT + u) * 5 + r + 1)
                            copy(AT[:, r * RB:(r + 1) * RB, ds((g * GT + u) * P, P)], turned[r][:, :, :]).then_inc(out, 1)

            @block.scalar
            def _(act):
                act.sem_inc(act_out, 3)
                move(act, lambda o, i: act.activation(o, i, ACT.Copy), 0, act_out, 3)

            @block.vector
            def _(dve):
                dve.memset(zeros[:, :], 0.0)
                dve.memset(ones[:, :], 1.0)
                dve.drain().then_inc(ready, 1)
                dve.sem_inc(free, GT)
                dve.sem_inc(dve_out, 2)
                move(dve, lambda o, i: dve.tensor_copy(o, i), 1, dve_out, 2)
                if outdeg is not None:
                    dve.wait_ge(ready, 2)
                    dve.tensor_scalar(outdeg[:, :], pdeg[:, :], -1.0, None, ALU.add)
                    dve.drain()


def split_rows(nc, source, width, parts, scale=None):
    with ExitStack() as ctx:
        m = Mem(nc, ctx)
        NB = 2 if width <= P else 1
        stage = m.sb("s_stage", [P, NB, GT, width])
        loaded = [m.sem(f"s_loaded{b}") for b in range(NB)]
        hi, rest, mid, rest2, lo = (m.sem(f"s_{n}") for n in ("hi", "rest", "mid", "rest2", "lo"))
        with nc.Block() as block:
            @block.sync
            def _(sp):
                for g in range(NG):
                    if g >= NB:
                        sp.wait_ge(lo, g - NB + 1)
                    sp.dma_start(stage[:, g % NB, :, :], rows(source, g * GT, GT)).then_inc(loaded[g % NB], 16)

            @block.scalar
            def _(act):
                for g in range(NG):
                    part = [parts[:, k, g * GT:(g + 1) * GT, :] for k in range(SPLIT)]
                    if scale is None:
                        act.wait_ge(loaded[g % NB], 16 * (g // NB + 1))
                    else:
                        act.wait_ge(rest, 2 * g + 1)
                    act.activation(part[0], stage[:, g % NB, :, :], ACT.Copy).then_inc(hi, 1)
                    act.wait_ge(rest, 2 * g + 2)
                    act.activation(part[1], stage[:, g % NB, :, :], ACT.Copy).then_inc(mid, 1)
                    act.wait_ge(rest2, g + 1)
                    act.activation(part[2], stage[:, g % NB, :, :], ACT.Copy).then_inc(lo, 1)

            @block.vector
            def _(dve):
                for g in range(NG):
                    part = [parts[:, k, g * GT:(g + 1) * GT, :] for k in range(SPLIT)]
                    s = stage[:, g % NB, :, :]
                    if scale is not None:
                        dve.wait_ge(loaded[g % NB], 16 * (g // NB + 1))
                        dve.tensor_tensor(s, s, scale[:, g * GT:(g + 1) * GT].unsqueeze(2).broadcast_to([P, GT, width]),
                                          ALU.mult).then_inc(rest, 1)
                    else:
                        dve.sem_inc(rest, 1)
                    dve.wait_ge(hi, g + 1)
                    dve.tensor_tensor(s, s, part[0], ALU.subtract).then_inc(rest, 1)
                    dve.wait_ge(mid, g + 1)
                    dve.tensor_tensor(s, s, part[1], ALU.subtract).then_inc(rest2, 1)


def sum_neighbours(pe, AT, parts, banks, f, g, half):
    for j in range(NT):
        for k in range(SPLIT):
            mm = pe.matmul(banks, parts[:, k, j, f * P:(f + 1) * P], AT[:, j, ds(g * GW + half * HW, HW)],
                           start=(j == 0 and k == 0), stop=(j == NT - 1 and k == SPLIT - 1))
    return mm


def norm_stats(dve, y, stats, mv, n):
    for u in range(n):
        dve.bn_stats(stats[:, u, :], y[:, u, :])
    dve.drain()
    for u in range(n):
        dve.bn_aggr(mv[:, u, :], stats[:, u, :])
    dve.drain()
    dve.tensor_scalar(mv[:, 0:n, 1], mv[:, 0:n, 1], 1e-5, None, ALU.add)
    return dve.drain()


def norm_apply(dve, y, mv, n):
    dve.reciprocal(mv[:, 0:n, 1], mv[:, 0:n, 1])
    dve.drain()
    for u in range(n):
        dve.tensor_scalar(y[:, u, :], y[:, u, :], mv[:, u, 0:1], mv[:, u, 1:2], ALU.subtract, ALU.mult)
    return dve.drain()


def gin_conv(nc, K, D, AT, tag, source, fb, w1, b1, w2, b2, ow, target, residual):
    with ExitStack() as ctx:
        m = Mem(nc, ctx)
        parts = m.sb(f"{tag}_parts", [P, SPLIT, NT, fb * P], BF16)
        split_rows(nc, source, fb * P, parts)
        w1s = m.sb(f"{tag}_w1", [P, fb, 2 * P])
        w2s = m.sb(f"{tag}_w2", [P, 2, ow])
        b1s = m.sb(f"{tag}_b1", [P, 2])
        b2s = m.sb(f"{tag}_b2", [P, ow])
        hid = m.sb(f"{tag}_hid", [P, 2, GW])
        y = m.sb(f"{tag}_y", [P, GT, ow])
        stats = m.sb(f"{tag}_stats", [P, GT, 6])
        mv = m.sb(f"{tag}_mv", [P, GT, 2])
        pa = [m.ps(f"{tag}_pa{i}", [P, BANK]) for i in range(4)]
        pb = [m.ps(f"{tag}_pb{i}", [P, BANK]) for i in range(4)]
        weights, resid, summed, sums_out, hidden, hidden_out, made, taken, var, dev, done, stored = (
            m.sem(f"{tag}_{n}") for n in ("weights", "resid", "summed", "sums_out", "hidden", "hidden_out", "made",
                                          "taken", "var", "dev", "done", "stored"))
        NS = 2 * fb
        with nc.Block() as block:
            @block.sync
            def _(sp):
                sp.sem_inc(stored, 16)
                sp.dma_start(w1s[:, :, :], w1.rearrange("(k p) n -> p k n", p=P)).then_inc(weights, 16)
                sp.dma_start(w2s[:, :, :], w2.rearrange("(k p) n -> p k n", p=P)).then_inc(weights, 16)
                sp.dma_start(b1s[:, :], b1).then_inc(weights, 16)
                sp.dma_start(b2s[:, :], b2.partition_broadcast(P)).then_inc(weights, 16)
                with sp.Fori(0, NG) as g:
                    if residual is not None:
                        sp.wait_ge(stored, g * 16 + 16)
                        sp.dma_start(y[:, :, :], rows(residual, g * GT, GT)).then_inc(resid, 16)
                    sp.wait_ge(done, g + 1)
                    sp.dma_start(rows(target, g * GT, GT), y[:, :, :]).then_inc(stored, 16)
                sp.wait_ge(stored, 16 * NG + 16)

            @block.tensor
            def _(pe):
                pe.wait_ge(weights, 64)
                with pe.Fori(0, NG) as g:
                    pe.wait_ge(taken, g * GT + 1)
                    for f in range(fb):
                        for half in range(2):
                            sum_neighbours(pe, AT, parts, pa[2 * f + half][:, 0:HW], f, g, half).then_inc(summed, 1)
                    pe.wait_ge(sums_out, NS * (g + 1))
                    for o in range(2):
                        for half in range(2):
                            for k in range(fb):
                                mm = pe.matmul(pb[2 * o + half][:, 0:HW], w1s[:, k, o * P:(o + 1) * P],
                                               hid[:, k, half * HW:(half + 1) * HW], start=(k == 0), stop=(k == fb - 1))
                    mm.then_inc(hidden, 1)
                    pe.wait_ge(hidden_out, 4 * (g + 1))
                    for u in range(GT):
                        if u == 4:
                            pe.wait_ge(taken, g * GT + 2)
                        for k in range(2):
                            mm = pe.matmul(pa[u % 4][:, 0:ow], hid[:, k, u * P:(u + 1) * P], w2s[:, k, :],
                                           start=(k == 0), stop=(k == 1))
                        mm.then_inc(made, 1)

            @block.scalar
            def _(act):
                act.wait_ge(weights, 64)
                with act.Fori(0, NG) as g:
                    act.wait_ge(hidden, g + 1)
                    for o in range(2):
                        for half in range(2):
                            act.activation(hid[:, o, half * HW:(half + 1) * HW], pb[2 * o + half][:, 0:HW], ACT.Relu,
                                           bias=b1s[:, o:o + 1]).then_inc(hidden_out, 1)
                    if residual is not None:
                        act.wait_ge(var, g + 1)
                        act.activation(mv[:, :, 1], mv[:, :, 1], ACT.Sqrt).then_inc(dev, 1)

            @block.vector
            def _(dve):
                dve.sem_inc(taken, 1)
                dve.wait_ge(weights, 64)
                with dve.Fori(0, NG) as g:
                    if residual is not None:
                        dve.wait_ge(resid, g * 16 + 16)
                        dve.tensor_tensor(y[:, :, :], y[:, :, :], b2s[:, :].unsqueeze(1).broadcast_to([P, GT, ow]), ALU.add)
                    for f in range(fb):
                        for half in range(2):
                            dve.wait_ge(summed, g * NS + 2 * f + half + 1)
                            dve.tensor_copy(hid[:, f, half * HW:(half + 1) * HW], pa[2 * f + half][:, 0:HW]).then_inc(sums_out, 1)
                    dve.drain()
                    if residual is None:
                        dve.wait_ge(stored, g * 16 + 16)
                    for u in range(GT):
                        dve.wait_ge(made, g * GT + u + 1)
                        dve.tensor_tensor(y[:, u, :], pa[u % 4][:, 0:ow], b2s[:, :] if residual is None else y[:, u, :],
                                          ALU.add).then_inc(taken, 1)
                    dve.drain()
                    if residual is None:
                        dve.tensor_scalar(y[:, :, :], y[:, :, :], 0.0, None, ALU.max).then_inc(done, 1)
                    else:
                        norm_stats(dve, y, stats, mv, GT).then_inc(var, 1)
                        dve.wait_ge(dev, g + 1)
                        norm_apply(dve, y, mv, GT).then_inc(done, 1)


HEADS = 4
PAIRS = HEADS // 2
SC = 400
SR = 2 * SC
ROUNDS = NP // SR
TB = 4
TR = -(-NT // TB)
FAR = 3.0e38


def attention(nc, K, D, source, fin, w, att_l, att_r, bias, ch, target, elu):
    FB = fin // P
    wd = HEADS * ch
    HB = wd // P
    per = P // ch
    with ExitStack() as ctx:
        m = Mem(nc, ctx)
        xwt = m.sb("t_xwt", [P, HB, NP])
        xw = m.sb("t_xw", [P, NT, HEADS, ch + 1])
        al = m.sb("t_al", [P, HEADS, NP])
        ar = m.sb("t_ar", [P, NT, HEADS])
        biasb = m.sb("t_bias", [P, wd])

        with ExitStack() as ctx2:
            m2 = Mem(nc, ctx2)
            ws = m2.sb("t_w", [P, FB, wd])
            attl = m2.sb("t_attl", [P, HB])
            attlb = m2.sb("t_attlb", [P, HB, P])
            attr = m2.sb("t_attr", [P, HB, per])
            x = m2.sb("t_x", [P, GT, fin])
            xt = m2.sb("t_xt", [P, FB, GW])
            ptr = [m2.ps(f"t_ptr{i}", [P, BANK]) for i in range(2)]
            pxt = [m2.ps(f"t_pxt{i}", [P, BANK]) for i in range(2)]
            pxw = [m2.ps(f"t_pxw{i}", [P, BANK]) for i in range(2)]
            par = m2.ps("t_par", [P, NT, HEADS])
            weights, loaded, turned, xt_out, free, xwt_made, xwt_out, xw_made, xw_out, al_made, al_out, ones_in, ar_made = (
                m2.sem(f"t_{n}") for n in ("weights", "loaded", "turned", "xt_out", "free", "xwt_made", "xwt_out",
                                           "xw_made", "xw_out", "al_made", "al_out", "ones_in", "ar_made"))
            NTURN = FB * 2
            with nc.Block() as block:
                @block.sync
                def _(sp):
                    sp.dma_start(ws[:, :, :], w.rearrange("(k p) n -> p k n", p=P)).then_inc(weights, 16)
                    sp.dma_start(attl[:, :], att_l).then_inc(weights, 16)
                    sp.dma_start(attr[:, :, :], att_r).then_inc(weights, 16)
                    sp.dma_start(biasb[:, :], bias.partition_broadcast(P)).then_inc(weights, 16)
                    with sp.Fori(0, NG) as g:
                        sp.wait_ge(turned, g * GT * FB + 1)
                        sp.dma_start(x[:, :, :], rows(source, g * GT, GT)).then_inc(loaded, 16)

                @block.tensor
                def _(pe):
                    pe.sem_inc(xw_made, 1)
                    pe.sem_inc(turned, 1)
                    pe.wait_ge(weights, 64)
                    with pe.Fori(0, NG) as g:
                        pe.wait_ge(loaded, g * 16 + 16)
                        for u in range(GT):
                            for k in range(FB):
                                i = u * FB + k
                                pe.wait_ge(xt_out, g * GT * FB + i + 1)
                                pe.transpose(ptr[i % 2][:, 0:P], x[:, u, k * P:(k + 1) * P], K["identf"][:, :]).then_inc(turned, 1)
                        pe.wait_ge(xt_out, (g + 1) * GT * FB + 2)
                        for hb in range(HB):
                            for half in range(2):
                                i = hb * 2 + half
                                pe.wait_ge(xwt_out, g * 2 * HB + i + 1)
                                for k in range(FB):
                                    mm = pe.matmul(pxt[i % 2][:, 0:HW], ws[:, k, hb * P:(hb + 1) * P],
                                                   xt[:, k, half * HW:(half + 1) * HW], start=(k == 0), stop=(k == FB - 1))
                                mm.then_inc(xwt_made, 1)
                        for u in range(GT):
                            pe.wait_ge(xw_out, g * GT + u + 1)
                            for k in range(FB):
                                mm = pe.matmul(pxw[u % 2][:, 0:wd], xt[:, k, u * P:(u + 1) * P], ws[:, k, :],
                                               start=(k == 0), stop=(k == FB - 1))
                            mm.then_inc(xw_made, 1)
                    pe.wait_ge(xwt_out, NG * 2 * HB + 2)
                    pe.wait_ge(xw_out, NG * GT + 2)
                    pe.wait_ge(ones_in, 1)
                    for h in range(HEADS):
                        hb, off = h // per, (h % per) * ch
                        for t in range(NT):
                            mm = pe.matmul(par[:, t, h:h + 1], xwt[:, hb, t * P:(t + 1) * P],
                                           attr[:, hb, h % per:h % per + 1], start=True, stop=True)
                        for q in range(NP // SC):
                            i = h * (NP // SC) + q
                            if i >= 2:
                                pe.wait_ge(al_out, i - 1)
                            pe.matmul(pxt[i % 2][:, 0:SC], attlb[off:off + ch, hb, :],
                                      xwt[off:off + ch, hb, q * SC:(q + 1) * SC], start=True, stop=True).then_inc(al_made, 1)
                    mm.then_inc(ar_made, 1)

                @block.scalar
                def _(act):
                    act.sem_inc(xwt_out, 2)
                    with act.Fori(0, NG) as g:
                        for hb in range(HB):
                            for half in range(2):
                                i = hb * 2 + half
                                act.wait_ge(xwt_made, g * 2 * HB + i + 1)
                                act.activation(xwt[:, hb, ds(g * GW + half * HW, HW)], pxt[i % 2][:, 0:HW],
                                               ACT.Copy).then_inc(xwt_out, 1)
                    for i in range(HEADS * NP // SC):
                        h, q = divmod(i, NP // SC)
                        act.wait_ge(al_made, i + 1)
                        act.activation(al[:, h, q * SC:(q + 1) * SC], pxt[i % 2][:, 0:SC], ACT.Copy).then_inc(al_out, 1)

                @block.vector
                def _(dve):
                    dve.sem_inc(xt_out, 2)
                    dve.sem_inc(xw_out, 2)
                    dve.memset(xw[:, :, :, ch:ch + 1], 1.0)
                    dve.wait_ge(weights, 64)
                    dve.tensor_copy(attlb[:, :, :], attl[:, :].unsqueeze(2).broadcast_to([P, HB, P]))
                    dve.drain().then_inc(ones_in, 1)
                    with dve.Fori(0, NG) as g:
                        for u in range(GT):
                            for k in range(FB):
                                i = u * FB + k
                                dve.wait_ge(turned, g * GT * FB + i + 2)
                                if i == 0:
                                    dve.wait_ge(xw_made, g * GT + 1)
                                dve.tensor_copy(xt[:, k, u * P:(u + 1) * P], ptr[i % 2][:, 0:P]).then_inc(xt_out, 1)
                        for u in range(GT):
                            dve.wait_ge(xw_made, g * GT + u + 2)
                            dve.tensor_copy(xw[:, ds(g * GT + u, 1), :, 0:ch],
                                            pxw[u % 2][:, 0:wd].rearrange("p (o h c) -> p o h c", o=1, h=HEADS)).then_inc(xw_out, 1)
                    dve.wait_ge(ar_made, 1)
                    dve.tensor_copy(ar[:, :, :], par[:, :, :])
                    dve.drain()

        counts = m.sb("t_counts", [P, 2, NP], BF16)
        absent = m.sb("t_absent", [P, NP], BF16)
        panel = [m.sb(f"t_panel{h}", [P, NP]) for h in range(HEADS)]
        panel_t = m.sb("t_panel_t", [P, NT, P])
        query = m.sb("t_query", [P, 2, P])
        top = m.sb("t_top", [P, HEADS, 2])
        inv = m.sb("t_inv", [P, HEADS])
        out = m.sb("t_out", [P, wd])
        neg = m.sb("t_neg", [P, wd])
        ps = [m.ps(f"t_ps{i}", [P, 2, BANK]) for i in range(2)]
        pt = [m.ps(f"t_pt{i}", [P, BANK]) for i in range(2)]
        po = [m.ps(f"t_po{i}", [P, BANK]) for i in range(2)]
        (loaded, query_in, scored, sigmoid, maxed, exps, weighted, turned, turned_out, applied, taken,
         low, low_exp, done, stored, act_passed, pool_passed, sp_passed) = (
            m.sem(f"t_{n}") for n in ("loaded", "query_in", "scored", "sigmoid", "maxed", "exps",
                                      "weighted", "turned", "turned_out", "applied", "taken", "low", "low_exp", "done",
                                      "stored", "act_passed", "pool_passed", "sp_passed"))

        def stages(eng, rounds, early, score, apply, weigh, finish, settle):
            def panels(t, last):
                for h in range(HEADS):
                    ahead = None if last and h + 3 >= HEADS else (t + (h + 3) // HEADS, (h + 3) % HEADS)
                    rounds((t, h), ahead, None if last else (t + 1, h))
                    if not last:
                        early(t + 1, h)
                    if h == 0:
                        settle(t)
                    if ahead:
                        score(*ahead)
                    apply(t, h)
                    if not last or h + 2 < HEADS:
                        weigh(t + (h + 2) // HEADS, (h + 2) % HEADS)
                finish(t)
            early(0, 0)
            for h in range(3):
                rounds(None, (0, h), (0, h + 1))
                early(0, h + 1)
                score(0, h)
                if h >= 1:
                    weigh(0, h - 1)
            with eng.Fori(0, NT - 1) as t:
                panels(t, False)
            panels(NT - 1, True)
            settle(NT)

        def alternate(turning, scoring, turn_round, score_round, first=0):
            for r in range(ROUNDS):
                if scoring and r >= first:
                    score_round(*scoring, r)
                if turning:
                    for q in (2 * r, 2 * r + 1):
                        if q < TR:
                            turn_round(*turning, q)

        def nothing(*_):
            return None

        with nc.Block() as block:
            @block.sync
            def _(sp):
                sp.sem_inc(loaded, 16)
                def load(t):
                    slot, row = sp.snap(t % 2), sp.snap(t * P)
                    sp.wait_ge(weighted, t * HEADS + 1)
                    sp.sem_inc(sp_passed, 1)
                    sp.wait_ge(loaded, t * 16 + 16)
                    sp.sem_inc(sp_passed, 1)
                    sp.dma_start(counts[:, ds(slot, 1), :],
                                 D["counts"][ds(row, P), :].rearrange("p (o s) -> p o s", o=1)).then_inc(loaded, 16)

                def store(t):
                    sp.wait_ge(done, t + 2)
                    sp.dma_start(target[ds(t * P, P), :], out[:, :]).then_inc(stored, 16)
                load(0)
                with sp.Fori(0, NT - 1) as t:
                    load(t + 1)
                    store(t)
                store(NT - 1)
                sp.wait_ge(stored, 16 * (NT + 1))

            @block.gpsimd
            def _(pool):
                def weigh(t, h):
                    n = t * HEADS + h
                    pool.wait_ge(exps, n + 1)
                    pool.sem_inc(pool_passed, 1)
                    pool.tensor_tensor(panel[h][:, :], panel[h][:, :],
                                       counts[:, ds(t % 2, 1), :].rearrange("p o s -> p (o s)"), ALU.mult).then_inc(weighted, 1)
                stages(pool, nothing, nothing, nothing, nothing, weigh, nothing, nothing)

            @block.tensor
            def _(pe):
                pe.sem_inc(applied, 1)
                pe.sem_inc(scored, 1)

                def score_round(t, h, r):
                    n = t * HEADS + h
                    if r == 0:
                        pe.wait_ge(query_in, n + 1)
                    hb, off = h // per, (h % per) * ch
                    pe.wait_ge(sigmoid, n * ROUNDS + r + 1)
                    for i in range(2):
                        c = r * SR + i * SC
                        mm = pe.matmul(ps[r % 2][:, i, 0:SC], query[off:off + ch, h % 2, :],
                                       xwt[off:off + ch, hb, c:c + SC], start=True, stop=True)
                    mm.then_inc(scored, 1)

                def turn_round(t, h, r):
                    n = t * HEADS + h
                    if r == 0:
                        pe.wait_ge(weighted, n + HEADS + 2)
                    pe.wait_ge(turned_out, n * TR + r + 1)
                    for i in range(min(TB, NT - r * TB)):
                        j = r * TB + i
                        mm = pe.transpose(pt[r % 2][:, i * P:(i + 1) * P], panel[h][:, j * P:(j + 1) * P],
                                          K["identf"][:, :])
                    mm.then_inc(turned, 1)

                def rounds(turning, scoring, following):
                    alternate(turning, scoring, turn_round, score_round, 1)

                def early(t, h):
                    score_round(t, h, 0)

                def apply(t, h):
                    n = t * HEADS + h
                    pe.wait_ge(turned_out, n * TR + TR + 2)
                    pe.wait_ge(taken, n + 1)
                    for j in range(NT):
                        mm = pe.matmul(po[h % 2][:, 0:ch + 1], panel_t[:, j, :], xw[:, j, h, :],
                                       start=(j == 0), stop=(j == NT - 1))
                    mm.then_inc(applied, 1)
                stages(pe, rounds, early, nothing, apply, nothing, nothing, nothing)

            @block.scalar
            def _(act):
                act.sem_inc(sigmoid, 2)
                act.sem_inc(turned_out, 2)

                def take_query(t, h):
                    hb = h // per
                    act.activation(query[:, h % 2, :].unsqueeze(1), xwt[:, hb:hb + 1, ds(t * P, P)],
                                   ACT.Copy).then_inc(query_in, 1)
                take_query(0, 0)

                def score_round(t, h, r):
                    n = t * HEADS + h
                    if r == 0:
                        act.wait_ge(turned, n * TR + 1)
                    act.wait_ge(scored, n * ROUNDS + r + 2)
                    act.activation(panel[h][:, r * SR:(r + 1) * SR].rearrange("p (i c) -> p i c", i=2),
                                   ps[r % 2][:, :, 0:SC], ACT.Sigmoid).then_inc(sigmoid, 1)

                def turn_round(t, h, r):
                    n = t * HEADS + h
                    if r == 0:
                        act.wait_ge(applied, n + 1)
                    b = min(TB, NT - r * TB)
                    act.wait_ge(turned, (n + HEADS - 1) * TR + r + 2)
                    act.activation(panel_t[:, r * TB:r * TB + b, :],
                                   pt[r % 2][:, 0:b * P].rearrange("p (b d) -> p b d", b=b), ACT.Copy).then_inc(turned_out, 1)

                def rounds(turning, scoring, following):
                    if following:
                        if scoring[1] or not isinstance(scoring[0], int):
                            act.wait_ge(scored, (scoring[0] * HEADS + scoring[1]) * ROUNDS + 1)
                            act.sem_inc(act_passed, 1)
                        take_query(*following)
                    alternate(turning, scoring, turn_round, score_round)

                def weigh(t, h):
                    n = t * HEADS + h
                    act.wait_ge(maxed, n + 1)
                    act.activation(panel[h][:, :], panel[h][:, :], ACT.Exp, bias=top[:, h, 1:2]).then_inc(exps, 1)

                def settle(t):
                    if elu:
                        act.wait_ge(low, t + 1)
                        act.activation(neg[:, :], neg[:, :], ACT.Exp).then_inc(low_exp, 1)
                stages(act, rounds, nothing, nothing, nothing, weigh, nothing, settle)

            @block.vector
            def _(dve):
                dve.sem_inc(weighted, HEADS + 1)
                dve.sem_inc(turned, (HEADS - 1) * TR + 1)
                dve.sem_inc(taken, 2)
                dve.sem_inc(stored, 16)
                dve.memset(out[:, :], 0.0)
                dve.memset(neg[:, :], 0.0)
                dve.drain().then_inc(low, 1)

                def score(t, h):
                    n = t * HEADS + h
                    if h == 0:
                        dve.wait_ge(loaded, t * 16 + 32)
                        dve.tensor_scalar(absent[:, :], counts[:, ds(t % 2, 1), :].rearrange("p o s -> p (o s)"),
                                          0.0, -BIG, ALU.is_equal, ALU.mult)
                    dve.wait_ge(sigmoid, n * ROUNDS + ROUNDS + 2)
                    dve.scalar_tensor_tensor(out=panel[h][:, :], in0=al[:, h, :],
                                             scalar=ar[:, ds(t, 1), h:h + 1].rearrange("p o h -> p (o h)"),
                                             in1=panel[h][:, :], op0=ALU.add, op1=ALU.mult)
                    dve.drain()
                    dve.tensor_tensor_reduce(panel[h][:, :], panel[h][:, :], absent[:, :], 1.0, -FAR, ALU.add, ALU.max,
                                             top[:, h, 0:1])
                    dve.drain()
                    dve.scalar_tensor_tensor(out=panel[h][:, :], in0=panel[h][:, :], scalar=0.2, in1=panel[h][:, :],
                                             op0=ALU.mult, op1=ALU.max)
                    dve.scalar_tensor_tensor(out=top[:, h, 1:2], in0=top[:, h, 0:1], scalar=0.2, in1=top[:, h, 0:1],
                                             op0=ALU.mult, op1=ALU.max)
                    dve.drain()
                    dve.tensor_scalar(top[:, h, 1:2], top[:, h, 1:2], -1.0, None, ALU.mult).then_inc(maxed, 1)

                def apply(t, h):
                    n = t * HEADS + h
                    if h == 0:
                        dve.wait_ge(stored, t * 16 + 16)
                    dve.wait_ge(applied, n + 2)
                    dve.tensor_scalar(inv[:, h:h + 1], po[h % 2][:, ch:ch + 1], 1e-16, None, ALU.add)
                    dve.drain()
                    dve.reciprocal(inv[:, h:h + 1], inv[:, h:h + 1])
                    dve.drain()
                    dve.scalar_tensor_tensor(out=out[:, h * ch:(h + 1) * ch], in0=po[h % 2][:, 0:ch],
                                             scalar=inv[:, h:h + 1], in1=biasb[:, h * ch:(h + 1) * ch],
                                             op0=ALU.mult, op1=ALU.add).then_inc(taken, 1)

                def finish(t):
                    dve.drain()
                    if elu:
                        dve.tensor_scalar(neg[:, :], out[:, :], 0.0, None, ALU.min).then_inc(low, 1)
                        dve.drain()
                        dve.tensor_scalar(out[:, :], out[:, :], 0.0, None, ALU.max)
                        dve.drain()

                def settle(t):
                    if elu:
                        dve.wait_ge(low_exp, t + 1)
                        dve.scalar_tensor_tensor(out=out[:, :], in0=neg[:, :], scalar=-1.0, in1=out[:, :],
                                                 op0=ALU.add, op1=ALU.add)
                        dve.drain()
                    dve.sem_inc(done, 1)
                stages(dve, nothing, nothing, score, apply, nothing, finish, settle)


def softmax_norm(nc, K, source, residual, target):
    with ExitStack() as ctx:
        m = Mem(nc, ctx)
        v = m.sb("u_v", [P, NT, P])
        x = m.sb("u_x", [P, NT, P])
        e = m.sb("u_e", [P, NT, P])
        top = m.sb("u_top", [P, NT])
        total = m.sb("u_total", [P, NT])
        stats = m.sb("u_stats", [P, NT, 6])
        mv = m.sb("u_mv", [P, NT, 2])
        loaded, step, act_step, stored = (m.sem(f"u_{n}") for n in ("loaded", "step", "act_step", "stored"))
        wide = [P, NT, P]
        with nc.Block() as block:
            @block.sync
            def _(sp):
                sp.dma_start(v[:, :, :], source.rearrange("(t p) f -> p t f", p=P)).then_inc(loaded, 16)
                sp.dma_start(x[:, :, :], residual.rearrange("(t p) f -> p t f", p=P)).then_inc(loaded, 16)
                sp.wait_ge(step, 4)
                sp.dma_start(target.rearrange("(t p) f -> p t f", p=P), x[:, :, :]).then_inc(stored, 16)
                sp.wait_ge(stored, 16)

            @block.scalar
            def _(act):
                act.wait_ge(step, 1)
                act.activation(e[:, :, :], v[:, :, :], ACT.Exp).then_inc(act_step, 1)
                act.wait_ge(step, 2)
                act.activation(total[:, :], total[:, :], ACT.Ln).then_inc(act_step, 1)
                act.wait_ge(step, 3)
                act.activation(mv[:, :, 1], mv[:, :, 1], ACT.Sqrt).then_inc(act_step, 1)

            @block.vector
            def _(dve):
                dve.wait_ge(loaded, 32)
                dve.tensor_reduce(top[:, :], v[:, :, :], AX_X, ALU.max)
                dve.drain()
                dve.tensor_tensor(v[:, :, :], v[:, :, :], top[:, :].unsqueeze(2).broadcast_to(wide), ALU.subtract)
                dve.drain().then_inc(step, 1)
                dve.tensor_tensor(x[:, :, :], x[:, :, :], v[:, :, :], ALU.add)
                dve.wait_ge(act_step, 1)
                dve.tensor_reduce(total[:, :], e[:, :, :], AX_X, ALU.add)
                dve.drain().then_inc(step, 1)
                dve.wait_ge(act_step, 2)
                dve.tensor_tensor(x[:, :, :], x[:, :, :], total[:, :].unsqueeze(2).broadcast_to(wide), ALU.subtract)
                dve.drain()
                norm_stats(dve, x, stats, mv, NT).then_inc(step, 1)
                dve.wait_ge(act_step, 3)
                norm_apply(dve, x, mv, NT).then_inc(step, 1)


GATES = 3


def gru_degrees(nc, K, AT, outdeg, from_scale, to_scale):
    Q = NP // SC
    with ExitStack() as ctx:
        m = Mem(nc, ctx)
        ones = m.sb("d_ones", [P, P], BF16)
        psum = [m.ps(f"d_psum{i}", [P, BANK]) for i in range(2)]
        ready, made, moved, clipped, rooted = (m.sem(f"d_{n}") for n in ("ready", "made", "moved", "clipped", "rooted"))
        with nc.Block() as block:
            @block.vector
            def _(dve):
                dve.memset(ones[:, :], 1.0)
                for t in range(NT):
                    block_ = AT[:, t, t * P:(t + 1) * P]
                    dve.tensor_tensor(block_, block_, K["identb"][:, :], ALU.subtract)
                dve.drain().then_inc(ready, 1)
                dve.tensor_scalar(from_scale[:, :], outdeg[:, :], 1.0, None, ALU.max)
                for q in range(Q):
                    dve.wait_ge(made, q + 1)
                    dve.tensor_scalar(to_scale[:, q * SC:(q + 1) * SC], psum[q % 2][:, 0:SC], 1.0, None, ALU.max).then_inc(moved, 1)
                dve.drain().then_inc(clipped, 1)
                dve.wait_ge(rooted, 2)
                dve.reciprocal(from_scale[:, :], from_scale[:, :])
                dve.reciprocal(to_scale[:, :], to_scale[:, :])
                dve.drain()

            @block.scalar
            def _(act):
                act.wait_ge(clipped, 1)
                act.activation(from_scale[:, :], from_scale[:, :], ACT.Sqrt).then_inc(rooted, 1)
                act.activation(to_scale[:, :], to_scale[:, :], ACT.Sqrt).then_inc(rooted, 1)

            @block.tensor
            def _(pe):
                pe.wait_ge(ready, 1)
                for q in range(Q):
                    if q >= 2:
                        pe.wait_ge(moved, q - 1)
                    for j in range(NT):
                        mm = pe.matmul(psum[q % 2][:, 0:SC], ones[:, :], AT[:, j, q * SC:(q + 1) * SC],
                                       start=(j == 0), stop=(j == NT - 1))
                    mm.then_inc(made, 1)


def gru_block(nc, K, D, AT, b, source, from_scale, to_scale, parts, target, residual):
    split_rows(nc, source, P, parts, from_scale)
    with ExitStack() as ctx:
        m = Mem(nc, ctx)
        wg = m.sb("r_wg", [P, P])
        wi = m.sb("r_wi", [P, GATES * P])
        bg = m.sb("r_bg", [P, 1])
        bi = m.sb("r_bi", [P, GATES])
        bh = m.sb("r_bh", [P, GATES])
        brz = m.sb("r_brz", [P, 2])
        summed = m.sb("r_summed", [P, GW])
        conv = m.sb("r_conv", [P, GW])
        reset = m.sb("r_reset", [P, GW])
        keep = m.sb("r_keep", [P, GW])
        cand = m.sb("r_cand", [P, GW])
        y = m.sb("r_y", [P, GT, P])
        stats = m.sb("r_stats", [P, GT, 6])
        mv = m.sb("r_mv", [P, GT, 2])
        pa = [m.ps(f"r_pa{i}", [P, BANK]) for i in range(2)]
        pg = [[m.ps(f"r_pg{c}{i}", [P, BANK]) for i in range(2)] for c in range(GATES)]
        (weights, biases, sums, sums_out, convs, convs_out, gates, gates_out, mixed, tanned, state, turned, taken,
         resid, var, dev, done, stored) = (
            m.sem(f"r_{n}") for n in ("weights", "biases", "sums", "sums_out", "convs", "convs_out", "gates",
                                      "gates_out", "mixed", "tanned", "state", "turned", "taken", "resid", "var", "dev",
                                      "done", "stored"))
        halves = [slice(i * HW, (i + 1) * HW) for i in range(2)]
        with nc.Block() as block:
            @block.sync
            def _(sp):
                sp.sem_inc(stored, 16)
                sp.dma_start(wg[:, :], D["gcn_w"][b * P:(b + 1) * P, :]).then_inc(weights, 16)
                sp.dma_start(wi[:, :], D["gru_w"][b * P:(b + 1) * P, :]).then_inc(weights, 16)
                sp.dma_start(bg[:, :], D["gcn_b"][b * P:(b + 1) * P, :]).then_inc(weights, 16)
                sp.dma_start(bi[:, :], D["gru_bi"][b * P:(b + 1) * P, :]).then_inc(weights, 16)
                sp.dma_start(bh[:, :], D["gru_bh"][b * P:(b + 1) * P, :]).then_inc(weights, 16)
                with sp.Fori(0, NG) as g:
                    if residual is not None:
                        sp.wait_ge(stored, g * 16 + 16)
                        sp.dma_start(y[:, :, :], rows(residual, g * GT, GT)).then_inc(resid, 16)
                    sp.wait_ge(done, g + 1)
                    sp.dma_start(rows(target, g * GT, GT), y[:, :, :]).then_inc(stored, 16)
                sp.wait_ge(stored, 16 * NG + 16)

            @block.tensor
            def _(pe):
                pe.sem_inc(turned, 1)
                pe.wait_ge(weights, 80)
                with pe.Fori(0, NG) as g:
                    pe.wait_ge(taken, g * GT + 1)
                    for i in range(2):
                        sum_neighbours(pe, AT, parts, pa[i][:, 0:HW], 0, g, i).then_inc(sums, 1)
                    for i in range(2):
                        pe.wait_ge(sums_out, g * 2 + i + 1)
                        pe.matmul(pg[2][i][:, 0:HW], wg[:, :], summed[:, halves[i]], start=True, stop=True).then_inc(convs, 1)
                    pe.wait_ge(convs_out, g * 2 + 2)
                    for c in range(GATES):
                        for i in range(2):
                            pe.matmul(pg[c][i][:, 0:HW], wi[:, c * P:(c + 1) * P], conv[:, halves[i]],
                                      start=True, stop=True).then_inc(gates, 1)
                    pe.wait_ge(state, g + 1)
                    for u in range(GT):
                        pe.transpose(pa[u // 4][:, u % 4 * P:(u % 4 + 1) * P], cand[:, u * P:(u + 1) * P],
                                     K["identf"][:, :]).then_inc(turned, 1)

            @block.scalar
            def _(act):
                act.wait_ge(biases, 1)
                with act.Fori(0, NG) as g:
                    for i in range(2):
                        act.wait_ge(convs, g * 2 + i + 1)
                        act.activation(conv[:, halves[i]], pg[2][i][:, 0:HW], ACT.Identity, bias=bg[:, 0:1]).then_inc(convs_out, 1)
                    for i in range(2):
                        act.wait_ge(gates, g * 6 + i + 1)
                        act.activation(reset[:, halves[i]], pg[0][i][:, 0:HW], ACT.Sigmoid, bias=brz[:, 0:1]).then_inc(gates_out, 1)
                    for i in range(2):
                        act.wait_ge(gates, g * 6 + 3 + i)
                        act.activation(keep[:, halves[i]], pg[1][i][:, 0:HW], ACT.Sigmoid, bias=brz[:, 1:2], scale=-1.0).then_inc(gates_out, 1)
                    act.wait_ge(mixed, g * 2 + 2)
                    act.activation(cand[:, :], cand[:, :], ACT.Tanh, bias=bi[:, 2:3]).then_inc(tanned, 1)
                    if residual is not None:
                        act.wait_ge(var, g + 1)
                        act.activation(mv[:, :, 1], mv[:, :, 1], ACT.Sqrt).then_inc(dev, 1)

            @block.vector
            def _(dve):
                dve.sem_inc(taken, 1)
                dve.wait_ge(weights, 80)
                dve.tensor_tensor(brz[:, :], bi[:, 0:2], bh[:, 0:2], ALU.add)
                dve.drain()
                dve.tensor_scalar(brz[:, 1:2], brz[:, 1:2], -1.0, None, ALU.mult)
                dve.drain().then_inc(biases, 1)
                with dve.Fori(0, NG) as g:
                    for i in range(2):
                        dve.wait_ge(sums, g * 2 + i + 1)
                        dve.tensor_tensor(summed[:, halves[i]], pa[i][:, 0:HW], to_scale[:, ds(g * GW + i * HW, HW)],
                                          ALU.mult).then_inc(sums_out, 1)
                    dve.drain()
                    dve.wait_ge(turned, g * GT + 1)
                    for i in range(2):
                        dve.wait_ge(gates_out, g * 4 + i + 1)
                        dve.wait_ge(gates, g * 6 + 5 + i)
                        dve.scalar_tensor_tensor(out=cand[:, halves[i]], in0=reset[:, halves[i]], scalar=bh[:, 2:3],
                                                 in1=pg[2][i][:, 0:HW], op0=ALU.mult, op1=ALU.add).then_inc(mixed, 1)
                    dve.wait_ge(gates_out, g * 4 + 4)
                    dve.wait_ge(tanned, g + 1)
                    dve.scalar_tensor_tensor(out=cand[:, :], in0=cand[:, :], scalar=0.0, in1=keep[:, :],
                                             op0=ALU.max, op1=ALU.mult).then_inc(state, 1)
                    if residual is None:
                        dve.wait_ge(stored, g * 16 + 16)
                    else:
                        dve.wait_ge(resid, g * 16 + 16)
                    for u in range(GT):
                        if u in (0, 4):
                            dve.wait_ge(turned, g * GT + min(u + 4, GT) + 1)
                        result = pa[u // 4][:, u % 4 * P:(u % 4 + 1) * P]
                        if residual is None:
                            dve.tensor_copy(y[:, u, :], result).then_inc(taken, 1)
                        else:
                            dve.tensor_tensor(y[:, u, :], result, y[:, u, :], ALU.add).then_inc(taken, 1)
                    if residual is not None:
                        dve.drain()
                        norm_stats(dve, y, stats, mv, GT).then_inc(var, 1)
                        dve.wait_ge(dev, g + 1)
                        norm_apply(dve, y, mv, GT)
                    dve.drain()
                    dve.sem_inc(done, 1)


RBF = 64
SUB = 4
STEPS = -(-NC // SUB)
NCS = STEPS * SUB


def edge_messages(nc, K, D, source):
    with ExitStack() as ctx:
        m = Mem(nc, ctx)
        W = SUB * P
        src = m.sb("e_src", [P, NCS], I32)
        dst = m.sb("e_dst", [P, NCS], I32)
        dump = m.sb("e_dump", [P, 1])
        before = m.sb("e_before", [P, P])
        zeros = m.sb("e_zeros", [P, NT + 1, P])
        w1 = m.sb("e_w1", [RBF, P])
        w2 = m.sb("e_w2", [P, P])
        b1 = m.sb("e_b1", [P, 1])
        b2 = m.sb("e_b2", [P, P])
        rbft = m.sb("e_rbft", [RBF, W])
        hid = m.sb("e_hid", [P, W])
        gate = m.sb("e_gate", [P, W])
        src_row = m.sb("e_src_row", [P, 2, W], I32)
        srcf = m.sb("e_srcf", [P, SUB])
        gap = m.sb("e_gap", [P, SUB])
        earlier = m.sb("e_earlier", [P, SUB])
        target = m.sb("e_target", [P, 2, SUB], I32)
        near = m.sb("e_near", [P, 2, SUB], I32)
        same = m.sb("e_same", [P, W])
        junk = m.sb("e_junk", [P, P])
        nodes = m.sb("e_nodes", [P, 2, SUB, P])
        msg = m.sb("e_msg", [P, SUB, P])
        merged = m.sb("e_merged", [P, SUB, P])
        ph, pw, pm = (m.ps(f"e_p{n}", [P, BANK]) for n in "hwm")
        tables, ready, zeroed, passed, sp_passed = (
            m.sem(f"e_{n}") for n in ("tables", "ready", "zeroed", "passed", "sp_passed"))
        (edges, hids, gated, hid_out, filt, filt_out, nears, sames, targets, msgs, merges,
         merges_out) = (
            m.sem(f"e_{n}") for n in ("edges", "hids", "gated", "hid_out", "filt", "filt_out", "nears",
                                      "sames", "targets", "msgs", "merges", "merges_out"))
        gathered = [[m.sem(f"e_gathered{s}{u}") for u in range(SUB)] for s in range(2)]
        scattered = [m.sem(f"e_scattered{u}") for u in range(SUB)]

        def in_pairs(eng, step):
            with eng.Fori(0, (STEPS - 1) // 2) as j:
                for s in range(2):
                    step(j * 2 + s, s, j)
            if (STEPS - 1) % 2:
                step(STEPS - 2, 0, STEPS // 2 - 1)

        with nc.Block() as block:
            @block.sync
            def _(sp):
                sp.sem_inc(edges, 16)
                sp.dma_start(src[:, :], D["src_pc2"]).then_inc(tables, 16)
                sp.dma_start(dst[:, :], D["dst_pc2"]).then_inc(tables, 16)
                sp.dma_start(w1[:, :], D["e_W1"]).then_inc(tables, 16)
                sp.dma_start(w2[:, :], D["e_W2"]).then_inc(tables, 16)
                sp.dma_start(b1[:, :], D["e_b1"]).then_inc(tables, 16)
                sp.dma_start(b2[:, :], D["e_b2"].partition_broadcast(P)).then_inc(tables, 16)
                with sp.Fori(0, STEPS) as i:
                    slot, row = sp.snap(i % 2), sp.snap(i * W)
                    sp.wait_ge(edges, i * 32 + 16)
                    sp.sem_inc(sp_passed, 1)
                    sp.wait_ge(hids, i + 1)
                    sp.wait_ge(sames, i + 1)
                    sp.sem_inc(sp_passed, 1)
                    sp.dma_start(rbft[:, :], D["edge_attr_t"][:, ds(row, W)]).then_inc(edges, 16)
                    sp.dma_start(src_row[:, ds(slot, 1), :].rearrange("p o e -> p (o e)"),
                                 D["src_row"][0:1, ds(row, W)].broadcast_to([P, W])).then_inc(edges, 16)

            @block.gpsimd
            def _(pool):
                pool.iota(dump[:, :], pattern=[[0, 1]], base=NP, channel_multiplier=1,
                          allow_small_or_imprecise_dtypes=True).then_inc(ready, 1)
                pool.memset(before[:, :], 1.0).then_inc(ready, 1)
                pool.wait_ge(ready, 2)
                pool.affine_select(out=before[:, :], in_=before[:, :], compare_op=ALU.is_gt, fill=0.0, base=0,
                                   pattern=[[-1, P]], channel_multiplier=1).then_inc(ready, 1)
                pool.wait_ge(zeroed, 1)
                for u in range(SUB):
                    pool.dma_start(D["acc"][u].rearrange("(t p) f -> p t f", p=P), zeros[:, :, :]).then_inc(scattered[u], 16)

                def gather(i, s):
                    pool.wait_ge(nears, i + 1)
                    for u in range(SUB):
                        pool.wait_ge(msgs, i * SUB + u + 1)
                        pool.sem_inc(passed, 1)
                        pool.indirect_dma_start(out=nodes[:, s, u, :], out_offset=None, in_=source,
                                                in_offset=bass.IndirectOffsetOnAxis(ap=near[:, s, u:u + 1], axis=0)).then_inc(gathered[s][u], 16)

                def scatter(i, s):
                    pool.wait_ge(targets, i + 1)
                    for u in range(SUB):
                        pool.wait_ge(merges_out, i * SUB + u + 2)
                        pool.wait_ge(scattered[u], i * 16 + 16)
                        pool.sem_inc(passed, 1)
                        pool.indirect_dma_start(out=D["acc"][u], in_=merged[:, u, :], in_offset=None, compute_op=ALU.add,
                                                out_offset=bass.IndirectOffsetOnAxis(ap=target[:, s, u:u + 1], axis=0)).then_inc(scattered[u], 16)
                def ahead(i, s, _):
                    gather(i + 1, 1 - s)
                    scatter(i, s)
                gather(0, 0)
                in_pairs(pool, ahead)
                scatter(STEPS - 1, (STEPS - 1) % 2)
                for u in range(SUB):
                    pool.wait_ge(scattered[u], 16 * STEPS + 16)

            @block.tensor
            def _(pe):
                pe.sem_inc(hids, 1)
                pe.sem_inc(filt, 1)
                pe.sem_inc(merges, 1)
                pe.wait_ge(tables, 96)

                def hide(i):
                    pe.wait_ge(edges, i * 32 + 48)
                    pe.wait_ge(hid_out, i + 1)
                    pe.matmul(ph[:, :], w1[:, :], rbft[:, :], start=True, stop=True).then_inc(hids, 1)

                def filter(i):
                    pe.wait_ge(hid_out, i + 2)
                    pe.wait_ge(filt_out, i + 1)
                    for u in range(SUB):
                        mm = pe.matmul(pw[:, u * P:(u + 1) * P], hid[:, u * P:(u + 1) * P], w2[:, :], start=True, stop=True)
                    mm.then_inc(filt, 1)

                def merge(i):
                    pe.wait_ge(sames, i + 2)
                    pe.wait_ge(merges_out, i * SUB + 1)
                    for u in range(SUB):
                        pe.wait_ge(msgs, (i + 2) * SUB + u + 1)
                        pe.matmul(pm[:, u * P:(u + 1) * P], same[:, u * P:(u + 1) * P], msg[:, u, :],
                                  start=True, stop=True).then_inc(merges, 1)
                hide(0)
                filter(0)
                with pe.Fori(0, STEPS - 1) as i:
                    hide(i + 1)
                    merge(i)
                    filter(i + 1)
                merge(STEPS - 1)

            @block.scalar
            def _(act):
                act.sem_inc(hid_out, 1)
                act.sem_inc(merges_out, 1)
                act.wait_ge(tables, 96)

                def hide(i):
                    act.wait_ge(filt, i + 1)
                    act.wait_ge(hids, i + 2)
                    act.activation(hid[:, :], ph[:, :], ACT.Silu, bias=b1[:, 0:1]).then_inc(hid_out, 1)

                def merge(i):
                    for u in range(SUB):
                        act.wait_ge(merges, (i + 1) * SUB + 1)
                        act.wait_ge(scattered[u], i * 16 + 16)
                        act.activation(merged[:, u, :], pm[:, u * P:(u + 1) * P], ACT.Copy).then_inc(merges_out, 1)
                hide(0)
                with act.Fori(0, STEPS - 1) as i:
                    hide(i + 1)
                    merge(i)
                merge(STEPS - 1)

            @block.vector
            def _(dve):
                dve.sem_inc(sames, 1)
                dve.sem_inc(filt_out, 1)
                dve.memset(zeros[:, :, :], 0.0).then_inc(zeroed, 1)
                dve.sem_inc(msgs, 2 * SUB)
                dve.wait_ge(tables, 96)
                dve.tensor_scalar(dst[:, :], dst[:, :], float(NP - 1), None, ALU.min)
                dve.drain()

                def near_of(i, s):
                    dve.tensor_copy(near[:, s, :], dst[:, ds(i * SUB, SUB)]).then_inc(nears, 1)
                near_of(0, 0)
                dve.wait_ge(ready, 3)

                def step(i, s, j):
                    dve.tensor_copy(srcf[:, :], src[:, ds(i * SUB, SUB)])
                    dve.drain()
                    dve.tensor_scalar(gap[:, :], srcf[:, :], dump[:, 0:1], -1.0, ALU.subtract, ALU.mult)
                    dve.wait_ge(edges, i * 32 + 48)
                    dve.wait_ge(merges, i * SUB + 1)
                    for u in range(SUB):
                        dve.tensor_scalar(same[:, u * P:(u + 1) * P],
                                          src_row[:, ds(i % 2, 1), u * P:(u + 1) * P].rearrange("p o e -> p (o e)"),
                                          srcf[:, u:u + 1], None, ALU.is_equal)
                    dve.drain().then_inc(sames, 1)
                    for u in range(SUB):
                        dve.tensor_tensor_reduce(junk[:, :], same[:, u * P:(u + 1) * P], before[:, :], 1.0, 0.0,
                                                 ALU.mult, ALU.add, earlier[:, u:u + 1])
                        dve.drain()
                    dve.scalar_tensor_tensor(out=gap[:, :], in0=earlier[:, :], scalar=0.0, in1=gap[:, :],
                                             op0=ALU.is_gt, op1=ALU.mult)
                    dve.drain()
                    dve.wait_ge(merges_out, i * SUB + 1)
                    dve.tensor_tensor(target[:, s, :], gap[:, :], srcf[:, :], ALU.add).then_inc(targets, 1)
                    dve.wait_ge(filt, i + 2)
                    dve.tensor_tensor(msg[:, :, :], pw[:, :].rearrange("p (u f) -> p u f", u=SUB),
                                      b2[:, :].unsqueeze(1).broadcast_to([P, SUB, P]), ALU.add).then_inc(filt_out, 1)
                    dve.drain()
                    for u in range(SUB):
                        dve.wait_ge(gathered[s][u], j * 16 + 16)
                        dve.tensor_tensor(msg[:, u, :], msg[:, u, :], nodes[:, s, u, :], ALU.mult).then_inc(msgs, 1)

                def prepared(i, s, j):
                    near_of(i + 1, 1 - s)
                    step(i, s, j)
                in_pairs(dve, prepared)
                step(STEPS - 1, (STEPS - 1) % 2, (STEPS - 1) // 2)


def node_update(nc, K, D, source, target):
    with ExitStack() as ctx:
        m = Mem(nc, ctx)
        w3 = m.sb("n_w3", [P, P])
        w4 = m.sb("n_w4", [P, P])
        b3 = m.sb("n_b3", [P, 1])
        b4 = m.sb("n_b4", [P, P])
        part = m.sb("n_part", [P, SUB, GT, P])
        x = m.sb("n_x", [P, GT, P])
        aggt = m.sb("n_aggt", [P, GW])
        hid = m.sb("n_hid", [P, GW])
        stats = m.sb("n_stats", [P, GT, 6])
        mv = m.sb("n_mv", [P, GT, 2])
        pt = [m.ps(f"n_pt{i}", [P, BANK]) for i in range(2)]
        ph = [m.ps(f"n_ph{i}", [P, BANK]) for i in range(2)]
        po = [m.ps(f"n_po{i}", [P, BANK]) for i in range(2)]
        weights, loaded, x_loaded, added, turned, turned_out, hids, hid_out, outs, var, dev, done, stored, sp_passed = (
            m.sem(f"n_{n}") for n in ("weights", "loaded", "x_loaded", "added", "turned", "turned_out", "hids", "hid_out", "outs",
                                      "var", "dev", "done", "stored", "sp_passed"))
        with nc.Block() as block:
            @block.sync
            def _(sp):
                sp.sem_inc(stored, 16)
                sp.dma_start(w3[:, :], D["e_W3"]).then_inc(weights, 16)
                sp.dma_start(w4[:, :], D["e_W4"]).then_inc(weights, 16)
                sp.dma_start(b3[:, :], D["e_b3"]).then_inc(weights, 16)
                sp.dma_start(b4[:, :], D["e_b4"].partition_broadcast(P)).then_inc(weights, 16)
                with sp.Fori(0, NG) as g:
                    sp.wait_ge(stored, g * 16 + 16)
                    for u in range(SUB):
                        sp.dma_start(part[:, u, :, :], rows(D["acc"][u], g * GT, GT)).then_inc(loaded, 16)
                    sp.dma_start(x[:, :, :], rows(source, g * GT, GT)).then_inc(x_loaded, 16)
                    sp.wait_ge(x_loaded, g * 16 + 16)
                    sp.sem_inc(sp_passed, 1)
                    sp.wait_ge(done, g + 1)
                    sp.dma_start(rows(target, g * GT, GT), x[:, :, :]).then_inc(stored, 16)
                sp.wait_ge(stored, 16 * NG + 16)

            @block.tensor
            def _(pe):
                pe.wait_ge(weights, 64)
                with pe.Fori(0, NG) as g:
                    pe.wait_ge(added, g + 1)
                    for u in range(GT):
                        mm = pe.transpose(pt[u // 4][:, u % 4 * P:(u % 4 + 1) * P], part[:, 0, u, :], K["identf"][:, :])
                    mm.then_inc(turned, 1)
                    pe.wait_ge(turned_out, g + 1)
                    for i in range(2):
                        pe.matmul(ph[i][:, 0:HW], w3[:, :], aggt[:, i * HW:(i + 1) * HW], start=True, stop=True).then_inc(hids, 1)
                    pe.wait_ge(hid_out, g * 2 + 2)
                    for u in range(GT):
                        mm = pe.matmul(po[u // 4][:, u % 4 * P:(u % 4 + 1) * P], hid[:, u * P:(u + 1) * P], w4[:, :],
                                       start=True, stop=True)
                    mm.then_inc(outs, 1)

            @block.scalar
            def _(act):
                act.wait_ge(weights, 64)
                with act.Fori(0, NG) as g:
                    for i in range(2):
                        act.wait_ge(hids, g * 2 + i + 1)
                        act.activation(hid[:, i * HW:(i + 1) * HW], ph[i][:, 0:HW], ACT.Silu, bias=b3[:, 0:1]).then_inc(hid_out, 1)
                    act.wait_ge(var, g + 1)
                    act.activation(mv[:, :, 1], mv[:, :, 1], ACT.Sqrt).then_inc(dev, 1)

            @block.vector
            def _(dve):
                dve.wait_ge(weights, 64)
                with dve.Fori(0, NG) as g:
                    dve.wait_ge(loaded, (g + 1) * SUB * 16)
                    for u in range(1, SUB):
                        dve.tensor_tensor(part[:, 0, :, :], part[:, 0, :, :], part[:, u, :, :], ALU.add)
                        dve.drain()
                    dve.sem_inc(added, 1)
                    dve.wait_ge(x_loaded, g * 16 + 16)
                    dve.tensor_scalar(x[:, :, :], x[:, :, :], 2.0, None, ALU.mult)
                    dve.drain()
                    dve.tensor_tensor(x[:, :, :], x[:, :, :], b4[:, :].unsqueeze(1).broadcast_to([P, GT, P]), ALU.add)
                    dve.wait_ge(turned, g + 1)
                    dve.tensor_copy(aggt[:, 0:4 * P], pt[0][:, :])
                    dve.tensor_copy(aggt[:, 4 * P:GW], pt[1][:, 0:P])
                    dve.drain().then_inc(turned_out, 1)
                    dve.wait_ge(outs, g + 1)
                    for u in range(GT):
                        dve.tensor_tensor(x[:, u, :], x[:, u, :], po[u // 4][:, u % 4 * P:(u % 4 + 1) * P], ALU.add)
                    dve.drain()
                    norm_stats(dve, x, stats, mv, GT).then_inc(var, 1)
                    dve.wait_ge(dev, g + 1)
                    norm_apply(dve, x, mv, GT).then_inc(done, 1)


LAYERS = 4


def gnn_program(nc, D):
    def scratch(name, shape, dt=F32):
        D[name] = nc.dram_tensor(name, shape, dt, kind="Internal").ap()

    scratch("counts", [NP, NP], BF16)
    for name in ("x1", "gat2", "x2", "x3"):
        scratch(name, [NP, P])
    for name in ("gin1", "gat1"):
        scratch(name, [NP, 2 * P])
    states = []
    for b in range(LAYERS - 1):
        scratch(f"state{b}", [NP, P])
        states.append(D[f"state{b}"])
    D["acc"] = [nc.dram_tensor(f"acc{u}", [NP + P, P], F32, kind="Internal").ap() for u in range(SUB)]

    with ExitStack() as ctx:
        m = Mem(nc, ctx)
        K = dict(identf=m.sb("identf", [P, P]), identb=m.sb("identb", [P, P], BF16),
                 bounds=m.sb("bounds", [1, NT + 1], I32), first_edge=m.sb("first_edge", [1, NT + 1]))
        make_constants(nc, K, D)
        build_counts(nc, K, D)
        with ExitStack() as ctx2:
            AT = Mem(nc, ctx2).sb("gin_counts", [P, NT, NP], BF16)
            load_counts(nc, K, D, AT)
            gin_conv(nc, K, D, AT, "g0", D["x"], 1, D["L0_W1a"], D["L0_b1a"], D["L0_W2a"], D["L0_b2a"], 2 * P,
                     D["gin1"], None)
            gin_conv(nc, K, D, AT, "g1", D["gin1"], 2, D["L0_W1b"], D["L0_b1b"], D["L0_W2b"], D["L0_b2b"], P,
                     D["x1"], D["x"])
        attention(nc, K, D, D["x1"], P, D["L1_W1"], D["L1_att_l1"], D["L1_att_r1"], D["L1_b1"], 2 * P // HEADS,
                  D["gat1"], True)
        attention(nc, K, D, D["gat1"], 2 * P, D["L1_W2"], D["L1_att_l2"], D["L1_att_r2"], D["L1_b2"], P // HEADS,
                  D["gat2"], False)
        softmax_norm(nc, K, D["gat2"], D["x1"], D["x2"])
        with ExitStack() as ctx2:
            m2 = Mem(nc, ctx2)
            outdeg = m2.sb("outdeg", [P, NT])
            AT = m2.sb("gru_counts", [P, NT, NP], BF16)
            load_counts(nc, K, D, AT, outdeg)
            to_scale = m2.sb("to_scale", [P, NP])
            from_scale = m2.sb("from_scale", [P, NT])
            parts = m2.sb("gru_parts", [P, SPLIT, NT, P], BF16)
            gru_degrees(nc, K, AT, outdeg, from_scale, to_scale)
            chain = [D["x2"], *states, D["x3"]]
            for b in range(LAYERS):
                gru_block(nc, K, D, AT, b, chain[b], from_scale, to_scale, parts, chain[b + 1],
                          D["x2"] if b == LAYERS - 1 else None)
        edge_messages(nc, K, D, D["x3"])
        node_update(nc, K, D, D["x3"], D["out"])


def laid_out(inputs):
    import numpy as np

    a = {n: np.asarray(v) for n, v in inputs.items()}

    def edges(v, fill, chunks):
        full = np.full(chunks * P, fill, v.dtype)
        full[:E] = v
        return full

    def by_chunk(v):
        return np.ascontiguousarray(v.reshape(-1, P).T)

    def padded(v, n):
        full = np.zeros((n, v.shape[1]), v.dtype)
        full[:v.shape[0]] = v
        return full

    def column(v):
        return np.ascontiguousarray(v.reshape(-1, P).T)

    def by_head(v):
        heads, ch = v.shape
        per = P // ch
        full = np.zeros((P, heads // per, per), v.dtype)
        for h in range(heads):
            full[h % per * ch:(h % per + 1) * ch, h // per, h % per] = v[h]
        return full

    src, dst = edges(a["src"], NP - 1, NCS), edges(a["dst"], PAD_DST, NCS)
    out = {
        "x": padded(a["x"], NP),
        "dst_pc": by_chunk(dst[:EP]), "src_pc": by_chunk(src[:EP]),
        "dst_pc2": by_chunk(dst), "src_pc2": by_chunk(src), "src_row": src.reshape(1, -1),
        "edge_attr_t": np.ascontiguousarray(padded(a["edge_attr_64"], NCS * P).T),
    }
    for n in ("W1a", "W2a", "b2a", "W1b", "W2b", "b2b"):
        out[f"L0_{n}"] = a[f"L0_gnn_{n}"]
    for n in ("b1a", "b1b"):
        out[f"L0_{n}"] = column(a[f"L0_gnn_{n}"])
    for n in ("W1", "W2", "b1", "b2"):
        out[f"L1_{n}"] = a[f"L1_gnn_{n}"]
    for n in ("1", "2"):
        out[f"L1_att_l{n}"] = column(a[f"L1_gnn_att_l{n}"])
        out[f"L1_att_r{n}"] = by_head(a[f"L1_gnn_att_r{n}"])
    out["gcn_w"] = a["L2_gnn_gcn_w"].reshape(LAYERS * P, P)
    out["gcn_b"] = a["L2_gnn_gcn_b"].reshape(LAYERS * P, 1)
    out["gru_w"] = np.ascontiguousarray(a["L2_gnn_gru_w_ih"].transpose(0, 2, 1)).reshape(LAYERS * P, GATES * P)
    for n, name in (("gru_bi", "b_ih"), ("gru_bh", "b_hh")):
        v = a[f"L2_gnn_gru_{name}"].reshape(LAYERS, GATES, P)
        out[n] = np.ascontiguousarray(v.transpose(0, 2, 1)).reshape(LAYERS * P, GATES)
    for n in ("W1", "W2", "W3", "W4", "b2", "b4"):
        out[f"e_{n}"] = a[f"L3_gnn_{n}"]
    for n in ("b1", "b3"):
        out[f"e_{n}"] = a[f"L3_gnn_{n}"].reshape(P, 1)
    return {n: np.ascontiguousarray(v) for n, v in out.items()}


def kernel(**inputs):
    import concourse.bacc as bacc
    from concourse.bass_utils import run_bass_kernel_spmd

    nc = bacc.Bacc("TRN2", target_bir_lowering=False, num_devices=1)
    arrays, D = {}, {}
    for name, v in laid_out(inputs).items():
        arrays[f"in_{name}"] = v
        D[name] = nc.dram_tensor(f"in_{name}", list(v.shape), mybir.dt.from_np(v.dtype), kind="ExternalInput").ap()
    D["out"] = nc.dram_tensor("out", [NP, P], F32, kind="ExternalOutput").ap()
    gnn_program(nc, D)
    r = run_bass_kernel_spmd(nc, [arrays], core_ids=[0])
    return r.results[0]["out"][:N_NODES]
```
